# Optimizing a Trainium2 kernel written in Bass

```python
import numpy as np
import jax
import jax.numpy as jnp

def _softmax(x, axis=-1):
    return jax.nn.softmax(x, axis=axis)

def _gelu(x):
    return jax.nn.gelu(x, approximate=True)

def _silu(x):
    return jax.nn.silu(x)

def _sigmoid(x):
    return jax.nn.sigmoid(x)

def _layernorm(x, axis=-1, eps=1e-05):
    m = jnp.mean(x, axis=axis, keepdims=True)
    v = jnp.var(x, axis=axis, keepdims=True)
    return (x - m) / jnp.sqrt(v + eps)

def _scatter_add(tgt, idx, src, axis=0):
    return tgt.at[idx].add(src)

def _segment_sum(src, seg, n):
    return jax.ops.segment_sum(src, seg, n)
kernel_name = 'mk_prb_d2_jaxref_r8_932597'

def setup_inputs(seed: int=0):
    np.random.seed(seed)
    _w = jnp.asarray

    def _L0_attn_setup():
        import jax, jax.numpy as jnp
        import numpy as np
        import math
        D_MODEL = 512
        NUM_HEADS = 32
        D_HEAD = D_MODEL // NUM_HEADS
        key = jax.random.key(seed)
        ks = jax.random.split(key, 9)
        B, N = (1, 256)
        s_d = 1.0 / math.sqrt(D_MODEL)
        x = jax.random.normal(ks[0], (B, N, D_MODEL), dtype=jnp.float32)
        Wq = jax.random.normal(ks[1], (D_MODEL, D_MODEL), dtype=jnp.float32) * s_d
        bq = jax.random.normal(ks[2], (D_MODEL,), dtype=jnp.float32) * s_d
        Wk = jax.random.normal(ks[3], (D_MODEL, D_HEAD), dtype=jnp.float32) * s_d
        bk = jax.random.normal(ks[4], (D_HEAD,), dtype=jnp.float32) * s_d
        Wv = jax.random.normal(ks[5], (D_MODEL, D_HEAD), dtype=jnp.float32) * s_d
        bv = jax.random.normal(ks[6], (D_HEAD,), dtype=jnp.float32) * s_d
        Wo = jax.random.normal(ks[7], (D_MODEL, D_MODEL), dtype=jnp.float32) * s_d
        bo = jax.random.normal(ks[8], (D_MODEL,), dtype=jnp.float32) * s_d
        return {'x': x, 'Wq': Wq, 'bq': bq, 'Wk': Wk, 'bk': bk, 'Wv': Wv, 'bv': bv, 'Wo': Wo, 'bo': bo}
    _L0_attn_in = _L0_attn_setup()

    def _L0_ffn_setup():
        import jax, jax.numpy as jnp
        import numpy as np
        H = 512
        I = 1376
        B, S = (2, 256)
        key = jax.random.key(seed)
        k1, k2, k3 = jax.random.split(key, 3)
        x = jax.random.normal(k1, (B, S, H), dtype=jnp.float32)
        w_gate_up = jax.random.normal(k2, (2 * I, H), dtype=jnp.float32) * 0.02
        w_down = jax.random.normal(k3, (H, I), dtype=jnp.float32) * 0.02
        return {'x': x, 'w_gate_up': w_gate_up, 'w_down': w_down}
    _L0_ffn_in = _L0_ffn_setup()

    def _L1_attn_setup():
        import jax, jax.numpy as jnp
        import numpy as np
        import math
        DIM = 512
        N_HEADS = 32
        N_KV_HEADS = 8
        HEAD_DIM = DIM // N_HEADS
        N_REP = N_HEADS // N_KV_HEADS
        ROPE_BASE = 10000.0

        def apply_rotary_emb(x):
            b, s, h, d = x.shape
            inv_freq = 1.0 / ROPE_BASE ** (jnp.arange(0, d, 2, dtype=jnp.float32) / d)
            pos = jnp.arange(s, dtype=jnp.float32)
            ang = pos[:, None] * inv_freq[None, :]
            cos = jnp.cos(ang)[None, :, None, :]
            sin = jnp.sin(ang)[None, :, None, :]
            xr = x.reshape(b, s, h, d // 2, 2)
            x0, x1 = (xr[..., 0], xr[..., 1])
            out = jnp.stack([x0 * cos - x1 * sin, x0 * sin + x1 * cos], axis=-1)
            return out.reshape(b, s, h, d)
        key = jax.random.key(seed)
        ks = jax.random.split(key, 5)
        sc = 1.0 / math.sqrt(DIM)
        return {'x': jax.random.normal(ks[0], (2, 256, DIM), dtype=jnp.float32), 'Wq': jax.random.normal(ks[1], (DIM, N_HEADS * HEAD_DIM), dtype=jnp.float32) * sc, 'Wk': jax.random.normal(ks[2], (DIM, N_KV_HEADS * HEAD_DIM), dtype=jnp.float32) * sc, 'Wv': jax.random.normal(ks[3], (DIM, N_KV_HEADS * HEAD_DIM), dtype=jnp.float32) * sc, 'Wo': jax.random.normal(ks[4], (N_HEADS * HEAD_DIM, DIM), dtype=jnp.float32) * sc}
    _L1_attn_in = _L1_attn_setup()

    def _L1_ffn_setup():
        import jax, jax.numpy as jnp
        import numpy as np
        B, S, D, O, E, R = (2, 512, 512, 512, 8, 16)
        TOP_K = 2
        SCALING = 32.0 / 16.0
        key = jax.random.key(seed)
        k = jax.random.split(key, 6)
        x = jax.random.normal(k[0], (B, S, D), dtype=jnp.float32)
        W_base = jax.random.normal(k[1], (O, D), dtype=jnp.float32) * 0.02
        b_base = jax.random.normal(k[2], (O,), dtype=jnp.float32) * 0.02
        W_router = jax.random.normal(k[3], (E, D), dtype=jnp.float32) * 0.01
        lora_A = jax.random.normal(k[4], (E, R, D), dtype=jnp.float32) * (1.0 / np.sqrt(D))
        lora_B = jax.random.normal(k[5], (E, O, R), dtype=jnp.float32) * 0.02
        return {'x': x, 'W_base': W_base, 'b_base': b_base, 'W_router': W_router, 'lora_A': lora_A, 'lora_B': lora_B}
    _L1_ffn_in = _L1_ffn_setup()
    _d = {'L0_attn_x': _L0_attn_in['x'], 'L0_attn_Wq': _L0_attn_in['Wq'], 'L0_attn_bq': _L0_attn_in['bq'], 'L0_attn_Wk': _L0_attn_in['Wk'], 'L0_attn_bk': _L0_attn_in['bk'], 'L0_attn_Wv': _L0_attn_in['Wv'], 'L0_attn_bv': _L0_attn_in['bv'], 'L0_attn_Wo': _L0_attn_in['Wo'], 'L0_attn_bo': _L0_attn_in['bo'], 'L0_ffn_w_gate_up': _L0_ffn_in['w_gate_up'], 'L0_ffn_w_down': _L0_ffn_in['w_down'], 'L1_attn_Wq': _L1_attn_in['Wq'], 'L1_attn_Wk': _L1_attn_in['Wk'], 'L1_attn_Wv': _L1_attn_in['Wv'], 'L1_attn_Wo': _L1_attn_in['Wo'], 'L1_ffn_W_base': _L1_ffn_in['W_base'], 'L1_ffn_b_base': _L1_ffn_in['b_base'], 'L1_ffn_W_router': _L1_ffn_in['W_router'], 'L1_ffn_lora_A': _L1_ffn_in['lora_A'], 'L1_ffn_lora_B': _L1_ffn_in['lora_B']}
    _x0 = _d['L0_attn_x']
    _d['L0_attn_x'] = jax.random.normal(jax.random.fold_in(jax.random.key(seed), 1), (2, 1024, 512), dtype=_x0.dtype)
    del _x0
    return _d

def reference(L0_attn_x, L0_attn_Wq, L0_attn_bq, L0_attn_Wk, L0_attn_bk, L0_attn_Wv, L0_attn_bv, L0_attn_Wo, L0_attn_bo, L0_ffn_w_gate_up, L0_ffn_w_down, L1_attn_Wq, L1_attn_Wk, L1_attn_Wv, L1_attn_Wo, L1_ffn_W_base, L1_ffn_b_base, L1_ffn_W_router, L1_ffn_lora_A, L1_ffn_lora_B):

    def _L0_attn_ref(x, Wq, bq, Wk, bk, Wv, bv, Wo, bo):
        import jax, jax.numpy as jnp
        import numpy as np
        import math
        D_MODEL = 512
        NUM_HEADS = 32
        D_HEAD = D_MODEL // NUM_HEADS
        B, N, D = x.shape
        H, d_h = (NUM_HEADS, D_HEAD)
        Q = (x @ Wq + bq).reshape(B, N, H, d_h)
        K = x @ Wk + bk
        V = x @ Wv + bv
        scale = 1.0 / math.sqrt(d_h)
        attn = jnp.einsum('bnhd,bkd->bhnk', Q, K) * scale
        attn = jax.nn.softmax(attn, axis=-1)
        out = jnp.einsum('bhnk,bkd->bnhd', attn, V).reshape(B, N, D)
        return out @ Wo + bo

    def _L0_ffn_ref(x, w_gate_up, w_down):
        import jax, jax.numpy as jnp
        import numpy as np
        H = 512
        I = 1376
        B, S = (2, 256)
        gate_up = jnp.einsum('bsh,oh->bso', x, w_gate_up)
        d = gate_up.shape[-1] // 2
        h = jax.nn.silu(gate_up[..., :d]) * gate_up[..., d:]
        return jnp.einsum('bsi,hi->bsh', h, w_down)

    def _L1_attn_ref(x, Wq, Wk, Wv, Wo):
        import jax, jax.numpy as jnp
        import numpy as np
        import math
        DIM = 512
        N_HEADS = 32
        N_KV_HEADS = 8
        HEAD_DIM = DIM // N_HEADS
        N_REP = N_HEADS // N_KV_HEADS
        ROPE_BASE = 10000.0

        def apply_rotary_emb(x):
            b, s, h, d = x.shape
            inv_freq = 1.0 / ROPE_BASE ** (jnp.arange(0, d, 2, dtype=jnp.float32) / d)
            pos = jnp.arange(s, dtype=jnp.float32)
            ang = pos[:, None] * inv_freq[None, :]
            cos = jnp.cos(ang)[None, :, None, :]
            sin = jnp.sin(ang)[None, :, None, :]
            xr = x.reshape(b, s, h, d // 2, 2)
            x0, x1 = (xr[..., 0], xr[..., 1])
            out = jnp.stack([x0 * cos - x1 * sin, x0 * sin + x1 * cos], axis=-1)
            return out.reshape(b, s, h, d)
        b, s, _ = x.shape
        xq = (x @ Wq).reshape(b, s, N_HEADS, HEAD_DIM)
        xk = (x @ Wk).reshape(b, s, N_KV_HEADS, HEAD_DIM)
        xv = (x @ Wv).reshape(b, s, N_KV_HEADS, HEAD_DIM)
        xq = apply_rotary_emb(xq)
        xk = apply_rotary_emb(xk)
        xk = jnp.repeat(xk, N_REP, axis=2)
        xv = jnp.repeat(xv, N_REP, axis=2)
        scores = jnp.einsum('bqhd,bkhd->bhqk', xq, xk) / math.sqrt(HEAD_DIM)
        causal = jnp.tril(jnp.ones((s, s), dtype=bool))
        scores = jnp.where(causal[None, None], scores, -jnp.inf)
        probs = jax.nn.softmax(scores.astype(jnp.float32), axis=-1).astype(xq.dtype)
        out = jnp.einsum('bhqk,bkhd->bqhd', probs, xv).reshape(b, s, N_HEADS * HEAD_DIM)
        return out @ Wo

    def _L1_ffn_ref(x, W_base, b_base, W_router, lora_A, lora_B):
        import jax, jax.numpy as jnp
        import numpy as np
        B, S, D, O, E, R = (2, 512, 512, 512, 8, 16)
        TOP_K = 2
        SCALING = 32.0 / 16.0
        d = x.shape[-1]
        n_experts = W_router.shape[0]
        xf = x.reshape(-1, d)
        logits = xf @ W_router.T
        probs = jax.nn.softmax(logits, axis=-1)
        topk_p, topk_i = jax.lax.top_k(probs, TOP_K)
        topk_p = topk_p / jnp.sum(topk_p, axis=-1, keepdims=True)
        w = jnp.sum(jax.nn.one_hot(topk_i, n_experts, dtype=xf.dtype) * topk_p[..., None], axis=1)
        h = jnp.einsum('td,erd->ter', xf, lora_A)
        lora_out = jnp.einsum('ter,eor,te->to', h, lora_B, w) * SCALING
        base = x @ W_base.T + b_base
        return base + lora_out.reshape(x.shape[:-1] + (W_base.shape[0],))
    x = L0_attn_x
    xn = _layernorm(x, axis=-1)
    x = x + _L0_attn_ref(xn, L0_attn_Wq, L0_attn_bq, L0_attn_Wk, L0_attn_bk, L0_attn_Wv, L0_attn_bv, L0_attn_Wo, L0_attn_bo) + _L0_ffn_ref(xn, L0_ffn_w_gate_up, L0_ffn_w_down)
    xn = _layernorm(x, axis=-1)
    x = x + _L1_attn_ref(xn, L1_attn_Wq, L1_attn_Wk, L1_attn_Wv, L1_attn_Wo) + _L1_ffn_ref(xn, L1_ffn_W_base, L1_ffn_b_base, L1_ffn_W_router, L1_ffn_lora_A, L1_ffn_lora_B)
    return x

_drawn_inputs = setup_inputs


def setup_inputs(seed=0):
    import zlib

    import numpy as np

    out = dict(_drawn_inputs(seed))
    spreads = {}
    factors = {'L0_attn_bq': 8.0, 'L0_attn_bk': 8.0, 'L1_ffn_b_base': 3.255}
    for name, (base, spread) in spreads.items():
        noise = np.random.default_rng([zlib.crc32(name.encode()), seed]).standard_normal(out[name].shape)
        drawn = base * np.exp(spread * noise) if base else spread * noise
        out[name] = jnp.asarray(drawn.astype(out[name].dtype))
    for name, factor in factors.items():
        out[name] = (out[name] * factor).astype(out[name].dtype)
    return out
```

```python
from contextlib import ExitStack

import concourse.bass as bass
from concourse import mybir

ALU = mybir.AluOpType
ACT = mybir.ActivationFunctionType
BF16 = mybir.dt.bfloat16
F32 = mybir.dt.float32
U32 = mybir.dt.uint32
AX_X = mybir.AxisListType.X

P = 128
B, N, D = 2, 1024, 512
T = B * N
TT = T // P
KC = D // P
CH = 512
NCH = T // CH
H, DH = 32, 16
HG = 4
NG = H // HG
KT = N // P
QC = N // CH
TPC = CH // P
F = 1376
FT = -(-F // P)
E, R = 8, 16
EPS = 1e-5
SCALE = 1.0 / DH ** 0.5
MASKED = -1e30
SLOTS = 4
ITERS = B * NG // SLOTS
SP_RING, P_RING, LAG = 3, 4, 2
PARTS = 3
ROWS = 6 * DH
MROWS = 2
NX = TPC * HG
XI = NX + 1


def width_f(j):
    return min(P, F - j * P)


def main_items(causal, qc):
    kts = TPC * (qc + 1) if causal else KT
    return [(kt, h, max(0, kt - TPC * qc) * P if causal else 0) for kt in range(kts) for h in range(HG)]


def max_width(causal, qc, qt):
    return (TPC * qc + qt + 1) * P if causal else N


def build(nc, x, wq0, bq0, wk0, bk0, wv0, bv0, wo0, bo0, wgu, wdn, wq1, wk1, wv1, wo1,
          wbase, bbase, wrt, la, lb, rcos, rsin, out):
    ctx = ExitStack()
    with ctx:
        def sb(name, shape, dt=F32):
            return ctx.enter_context(nc.sbuf_tensor(name, shape, dt))

        def sem(name):
            return ctx.enter_context(nc.semaphore(name))

        qparts = [nc.dram_tensor(f"qparts{l}", [B * H, PARTS * DH, N], BF16, kind="Internal").ap() for l in (0, 1)]
        kparts = [nc.dram_tensor(f"kparts{l}", [B * kv, PARTS * DH, N], BF16, kind="Internal").ap()
                  for l, kv in ((0, 1), (1, NG))]
        numer = [nc.dram_tensor(f"numer{l}", [B * H, DH, N], F32, kind="Internal").ap() for l in (0, 1)]
        denom = [nc.dram_tensor(f"denom{l}", [B * H, N], F32, kind="Internal").ap() for l in (0, 1)]

        acc = sb("acc", [P, TT, D])
        xnT = sb("xnT", [P, KC, T])
        w_q = sb("w_q", [P, KC, D])
        w_kv = sb("w_kv", [P, KC, 256])
        w_o = sb("w_o", [P, KC, D])
        bias_q = sb("bias_q", [P, KC])
        bias_k = sb("bias_k", [DH, 1])
        bias_v = sb("bias_v", [P, DH])
        bias_o = sb("bias_o", [P, D])
        v_all = sb("v_all", [P, B * NG, KT, DH + 1])
        ident = sb("ident", [P, P])
        identb = sb("identb", [P, P], BF16)
        mask_kq = sb("mask_kq", [P, P], BF16)
        mask_qk = sb("mask_qk", [P, P], BF16)
        stats = sb("stats", [P, TT, 6])
        mv = sb("mv", [P, TT, 2])
        var = sb("var", [P, TT])
        std = sb("std", [P, TT])
        rstd = sb("rstd", [P, TT])
        nwt = sb("nwt", [P, TT])
        AR = 20 * 1024
        arena = sb("arena", [P, AR])

        used = [0]

        def region(cols, dt=F32, parts=P):
            a = used[0]
            used[0] += cols
            assert used[0] <= AR, used[0]
            v = arena[0:parts, a:a + cols]
            return v if dt == F32 else v.bitcast(dt)

        xn = [region(D) for _ in range(2)]
        used[0] = 2 * D
        w_gu = region(KC * 2 * F).rearrange("p (k f) -> p k f", k=KC)
        w_dn = region(FT * D).rearrange("p (j d) -> p j d", j=FT)
        sil = [region(CH) for _ in range(2)]
        hid = [region(CH) for _ in range(2)]
        used[0] = 2 * D
        w_base = region(KC * D).rearrange("p (k f) -> p k f", k=KC)
        w_ar = region(KC * (E * R + E)).rearrange("p (k f) -> p k f", k=KC)
        w_lb = region(D)
        hl = region(TT * (E * R + E)).rearrange("p (t f) -> p t f", t=TT)
        hw = region(TT * E * R).rearrange("p (t f) -> p t f", t=TT)
        hwT = region(TT * P).rearrange("p (t f) -> p t f", t=TT)
        top = region(TT * 8).rearrange("p (t f) -> p t f", t=TT)
        topi = region(TT * 8, U32).rearrange("p (t f) -> p t f", t=TT)
        topf = region(TT * 2).rearrange("p (t f) -> p t f", t=TT)
        gap = region(TT)
        egap = region(TT)
        esum = region(TT)
        winv = region(TT)
        wt1 = region(TT)
        wt2 = region(TT)
        gate1 = region(TT * E).rearrange("p (t f) -> p t f", t=TT)
        gate2 = region(TT * E).rearrange("p (t f) -> p t f", t=TT)
        gate = region(TT * E).rearrange("p (t f) -> p t f", t=TT)
        iota8 = region(E)
        NQ = KC + 1
        used[0] = 0
        q32 = [region(CH) for _ in range(NQ)]
        rest = [region(CH) for _ in range(NQ)]
        part = [region(PARTS * CH // 2, BF16).rearrange("p (s q) -> p s q", s=PARTS) for _ in range(NQ)]
        rope_cos = region(N)
        rope_sin = region(N)
        used[0] = 0
        q_slot = [region(HG * N // 2, BF16).rearrange("p (c h q) -> p c h q", c=QC, h=HG) for _ in range(SLOTS)]
        k_slot = [region(N // 2, BF16) for _ in range(SLOTS)]
        v_slot = [region(KT * (DH + 1)).rearrange("p (k d) -> p k d", k=KT) for _ in range(SLOTS)]
        prob = [region(CH) for _ in range(P_RING)]
        o_sb = [region(CH) for _ in range(QC)]
        maxes = [region(NX) for _ in range(QC)]
        negm = [region(MROWS * P // 2, BF16).rearrange("p (s q) -> p s q", s=MROWS) for _ in range(QC)]
        used[0] = 0
        den = [region(N) for _ in range(2)]
        res = [region(D) for _ in range(4)]

        ps = ctx.enter_context(nc.psum_tensor("ps", [P, 8 * CH], F32))

        def bank(i, n=1):
            return ps[:, i * CH:(i + n) * CH]

        def sems(l):
            names = ("eps_done sqrt_done xn_ready xn_T xnT_ready acc_biased "
                     "gu_ready silu_done hid_done y_ready y_evac "
                     "hl_ready hl_sb gap_done egap_done "
                     "hw_done hwT_ready hwT_sb b_ready b_evac "
                     "q_ready q32_ready hi_done rest_ready mid_done lo_done v_ready v_done "
                     "v_slot_ready s_ready p_ready pv_done o_copied x_ready x_done mhi_done m_ready "
                     "den_inv on_ready y2_ready y2_evac").split()
            S = {n: sem(f"{n}_{l}") for n in names}
            S["q_out"] = [sem(f"q_out{m}_{l}") for m in range(NQ)]
            S["slot_in"] = [sem(f"slot_in{u}_{l}") for u in range(SLOTS)]
            S["m_in"] = [sem(f"m_in{c}_{l}") for c in range(QC)]
            S["o_out"] = [sem(f"o_out{c}_{l}") for c in range(QC)]
            S["num_in"] = [sem(f"num_in{i}_{l}") for i in range(B * KC)]
            S["stored"] = [sem(f"stored{i}_{l}") for i in range(4 * l)]
            S["wf_in"] = sem(f"wf_in_{l}")
            S["wp_in"] = sem(f"wp_in_{l}")
            return S

        L = [sems(0), sems(1)]
        x_in = sem("x_in")
        rope_in = sem("rope_in")
        swap = [i ^ 1 for i in range(32)]
        const_a = sem("const_a")
        const_b = sem("const_b")
        iota_done = sem("iota_done")
        dve_chain = sem("dve_chain")

        KVW = [DH, NG * DH]
        per_group = [sum(len(main_items(l == 1, c)) for c in range(QC)) for l in (0, 1)]

        block = ctx.enter_context(nc.Block())

        @block.sync
        def _(sp):
            sp.dma_start(acc[:, :, :], x.rearrange("(t p) d -> p t d", p=P)).then_inc(x_in, 16)

            def load_projections(l):
                S = L[l]
                wq, wk, wv, wo = ((wq0, wk0, wv0, wo0), (wq1, wk1, wv1, wo1))[l]
                kw = KVW[l]
                r = "(k p) n -> p k n"
                sp.dma_start(w_q[:, :, :], wq.rearrange(r, p=P)).then_inc(S["wp_in"], 16)
                sp.dma_start(w_kv[:, :, 0:kw], wk.rearrange(r, p=P)).then_inc(S["wp_in"], 16)
                sp.dma_start(w_kv[:, :, kw:2 * kw], wv.rearrange(r, p=P)).then_inc(S["wp_in"], 16)
                sp.dma_start(w_o[:, :, :], wo.rearrange(r, p=P)).then_inc(S["wp_in"], 16)
                if l == 0:
                    sp.dma_start(bias_q[:, :], bq0).then_inc(S["wp_in"], 16)
                    sp.dma_start(bias_k[:, :], bk0.rearrange("(p a) -> p a", a=1)).then_inc(S["wp_in"], 16)
                    sp.dma_start(bias_v[:, :], bv0.partition_broadcast(P)).then_inc(S["wp_in"], 16)
                    sp.dma_start(bias_o[:, :], bo0.partition_broadcast(P)).then_inc(S["wp_in"], 16)
                else:
                    sp.dma_start(bias_o[:, :], bbase.partition_broadcast(P)).then_inc(S["wp_in"], 16)

            def load_ffn0():
                S = L[0]
                sp.dma_start(w_gu, wgu.rearrange("(k p) n -> p k n", p=P)).then_inc(S["wf_in"], 16)
                sp.dma_start(w_dn[:, 0:FT - 1, :], wdn[0:(FT - 1) * P, :].rearrange("(j p) n -> p j n", p=P)).then_inc(S["wf_in"], 16)
                sp.dma_start(w_dn[0:width_f(FT - 1), FT - 1, :], wdn[(FT - 1) * P:F, :]).then_inc(S["wf_in"], 16)

            def load_ffn1():
                S = L[1]
                r = "(k p) n -> p k n"
                sp.dma_start(w_base, wbase.rearrange(r, p=P)).then_inc(S["wf_in"], 16)
                sp.dma_start(w_ar[:, :, 0:E * R], la.rearrange(r, p=P)).then_inc(S["wf_in"], 16)
                sp.dma_start(w_ar[:, :, E * R:E * R + E], wrt.rearrange(r, p=P)).then_inc(S["wf_in"], 16)
                sp.dma_start(w_lb, lb).then_inc(S["wf_in"], 16)

            def store_parts(l):
                S = L[l]
                with sp.Fori(0, B) as b:
                    with sp.Fori(0, QC) as cc:
                        for m in range(NQ):
                            sp.wait_ge(S["lo_done"], (b * QC + cc) * NQ + m + 1)
                            for s in range(PARTS):
                                if m < KC:
                                    dst = qparts[l][bass.ds(b * H + m * (P // DH), P // DH), s * DH:(s + 1) * DH, bass.ts(cc, CH)]
                                    src = part[m][:, s, :]
                                elif l == 0:
                                    dst = kparts[l][bass.ds(b, 1), s * DH:(s + 1) * DH, bass.ts(cc, CH)]
                                    src = part[m][0:DH, s, :]
                                else:
                                    dst = kparts[l][bass.ds(b * NG, NG), s * DH:(s + 1) * DH, bass.ts(cc, CH)]
                                    src = part[m][:, s, :]
                                sp.dma_start(dst, src).then_inc(S["q_out"][m], 16)
                for m in range(NQ):
                    sp.wait_ge(S["q_out"][m], 16 * PARTS * NCH)

            def load_slot(l, it, u):
                S = L[l]
                n = it * SLOTS + u
                q = qparts[l][bass.ds(n * HG, HG), :, :] if not isinstance(n, int) else qparts[l][n * HG:(n + 1) * HG, :, :]
                kn = n if l else it // (ITERS // B)
                k = kparts[l][bass.ds(kn, 1), :, :]
                for row, rows in ((0, 3 * DH), (3 * DH, 2 * DH), (5 * DH, DH)):
                    for c in range(QC):
                        sp.dma_start(q_slot[u][row:row + rows, c, :, :],
                                     q[:, 0:rows, c * CH:(c + 1) * CH].rearrange("h r q -> r h q")).then_inc(S["slot_in"][u], 16)
                for row, s in ((0, 0), (1, 0), (2, 0), (3, 1), (4, 1), (5, 2)):
                    sp.dma_start(k_slot[u][row * DH:(row + 1) * DH, :],
                                 k[:, s * DH:(s + 1) * DH, :].rearrange("o d q -> (o d) q")).then_inc(S["slot_in"][u], 16)

            def max_rows(l, u, c, m):
                S = L[l]
                sp.wait_ge(S["m_ready"], m + 1)
                for s in range(MROWS):
                    sp.dma_start(q_slot[u][ROWS + s:ROWS + s + 1, c, :, :].rearrange("o h (t q) -> o (h t) q", q=P),
                                 negm[c][0:NX, s, :]).then_inc(S["m_in"][c], 16)

            def store_o(l, it, u, c):
                S = L[l]
                n = it * SLOTS + u
                sp.wait_ge(S["o_copied"], n * QC + c + 2)
                for h in range(HG):
                    sp.dma_start(numer[l][bass.ds(n * HG + h, 1), :, c * CH:(c + 1) * CH].rearrange("o d q -> (o d) q"),
                                 o_sb[c][32 * h:32 * h + DH, :]).then_inc(S["o_out"][c], 16)
                sp.dma_start(denom[l][bass.ds(n * HG, HG), c * CH:(c + 1) * CH],
                             o_sb[c][DH:P:32, :]).then_inc(S["o_out"][c], 16)

            def attention(l):
                S = L[l]
                for u in range(SLOTS - 1):
                    load_slot(l, 0, u)
                for c in range(QC):
                    max_rows(l, 0, c, c)

                def step(it, u, last):
                    n = it * SLOTS + u
                    final = last and u == SLOTS - 1
                    if not (last and u > 0):
                        v = (u + SLOTS - 1) % SLOTS
                        sp.wait_ge(S["pv_done"], n * per_group[l] + P_RING)
                        load_slot(l, it if u == 0 else it + 1, v)
                    for c in range(QC):
                        if not final:
                            max_rows(l, (u + 1) % SLOTS, c, (n + 1) * QC + c)
                        store_o(l, it, u, c)

                with sp.Fori(0, ITERS - 1) as it:
                    for u in range(SLOTS):
                        step(it, u, False)
                for u in range(SLOTS):
                    step(ITERS - 1, u, True)
                for c in range(QC):
                    sp.wait_ge(S["o_out"][c], 80 * B * NG + 16)

            def load_output(l):
                S = L[l]
                for i in range(B * KC):
                    b, t = divmod(i, KC)
                    h0 = b * H + t * (P // DH)
                    if i >= 2:
                        sp.wait_ge(S["on_ready"], i - 1)
                    sp.dma_start(xnT[:, t, b * N:(b + 1) * N], numer[l][h0:h0 + P // DH, :, :].rearrange("h d q -> (h d) q")).then_inc(S["num_in"][i], 16)
                    for h in range(P // DH):
                        sp.dma_start(den[i % 2][h * DH:(h + 1) * DH, :],
                                     denom[l][h0 + h, :].partition_broadcast(DH)).then_inc(S["num_in"][i], 16)

            load_projections(0)
            load_ffn0()
            for l in (0, 1):
                S = L[l]
                if l == 1:
                    sp.wait_ge(L[0]["y2_ready"], TT)
                    sp.wait_ge(L[0]["y2_evac"], TT)
                    load_projections(1)
                    load_ffn1()
                if l == 1:
                    sp.wait_ge(S["b_ready"], TT)
                    sp.dma_start(rope_cos, rcos).then_inc(rope_in, 16)
                    sp.dma_start(rope_sin, rsin).then_inc(rope_in, 16)
                store_parts(l)
                attention(l)
                load_output(l)
            S = L[1]
            for t in range(TT):
                sp.wait_ge(S["y2_evac"], t + 1)
                sp.dma_start(out[t * P:(t + 1) * P, :], res[t % 4]).then_inc(S["stored"][t % 4], 16)
            for s in S["stored"]:
                sp.wait_ge(s, 16 * TT // 4)

        @block.gpsimd
        def _(pool):
            pool.memset(ident[:, :], 0.0).then_inc(const_a, 1)
            pool.memset(identb[:, :], 0.0).then_inc(const_a, 1)
            pool.memset(mask_kq[:, :], 0.0).then_inc(const_a, 1)
            pool.memset(mask_qk[:, :], 0.0).then_inc(const_a, 1)
            pool.memset(v_all[:, :, :, DH:DH + 1], 1.0).then_inc(const_a, 1)
            pool.wait_ge(const_a, 5)
            for m in (ident, identb):
                pool.affine_select(out=m[:, :], in_=m[:, :], compare_op=ALU.not_equal, fill=1.0, base=0,
                                   pattern=[[-1, P]], channel_multiplier=1).then_inc(const_b, 1)
            pool.affine_select(out=mask_kq[:, :], in_=mask_kq[:, :], compare_op=ALU.is_ge, fill=MASKED, base=0,
                               pattern=[[1, P]], channel_multiplier=-1).then_inc(const_b, 1)
            pool.affine_select(out=mask_qk[:, :], in_=mask_qk[:, :], compare_op=ALU.is_ge, fill=MASKED, base=0,
                               pattern=[[-1, P]], channel_multiplier=1).then_inc(const_b, 1)
            for l in (0, 1):
                S = L[l]
                pool.wait_ge(S["wp_in"], 16 * (8 if l == 0 else 5))
                for t in range(TT):
                    pool.wait_ge(S["xn_ready"], t + 1)
                    pool.tensor_tensor(acc[:, t, :], acc[:, t, :], bias_o[:, :], ALU.add).then_inc(S["acc_biased"], 1)
                if l == 1:
                    pool.iota(topi[:, 0, :], pattern=[[1, E]], base=0, channel_multiplier=0).then_inc(iota_done, 1)
                    pool.wait_ge(iota_done, 1)
                    pool.tensor_copy(iota8, topi[:, 0, :]).then_inc(iota_done, 1)
                for c in range(NCH):
                    for m in range(NQ):
                        rows = DH if (m == KC and l == 0) else P
                        pool.wait_ge(S["rest_ready"], c * NQ + m + 1)
                        pool.tensor_copy(part[m][0:rows, 1, :], rest[m][0:rows, :]).then_inc(S["mid_done"], 1)
                        pool.wait_ge(S["mid_done"], c * NQ + m + 1)
                        pool.tensor_tensor(part[m][0:rows, 2, :], rest[m][0:rows, :], part[m][0:rows, 1, :],
                                           ALU.subtract).then_inc(S["lo_done"], 1)
                pool.wait_ge(S["v_done"], TT)
                pool.wait_ge(S["lo_done"], NCH * NQ)
                for m in range(NQ):
                    pool.wait_ge(S["q_out"][m], 16 * PARTS * NCH)

                def v_stage(it, u):
                    n = it * SLOTS + u
                    vn = n if l else it // (ITERS // B)
                    pool.tensor_copy(v_slot[u], v_all[:, vn, :, :]).then_inc(S["v_slot_ready"], 1)

                for u in range(SLOTS):
                    pool.memset(k_slot[u][ROWS:ROWS + MROWS, :], 1.0).then_inc(S["v_slot_ready"], 1)
                pool.wait_ge(S["v_slot_ready"], SLOTS)
                for u in range(SLOTS):
                    v_stage(0, u)
                for it in range(1, ITERS):
                    for u in range(SLOTS):
                        pool.wait_ge(S["pv_done"], (it * SLOTS + u - SLOTS + 1) * per_group[l] + P_RING)
                        v_stage(it, u)

        @block.scalar
        def _(act):
            for l in (0, 1):
                S = L[l]
                act.wait_ge(S["eps_done"], 1)
                act.activation(std[:, :], var[:, :], ACT.Sqrt).then_inc(S["sqrt_done"], 1)
                with act.Fori(0, TT // 2) as i:
                    for j in range(2):
                        act.wait_ge(S["xn_T"], i * 2 + j + 1)
                        act.activation(xnT[:, :, bass.ts(i * 2 + j, P)], bank(j).rearrange("p (k q) -> p k q", k=KC), ACT.Copy).then_inc(S["xnT_ready"], 1)
                if l == 0:
                    with act.Fori(0, NCH) as c:
                        for j in range(FT):
                            w = width_f(j)
                            act.wait_ge(S["gu_ready"], c * FT + j + 1)
                            act.activation(sil[j % 2][0:w, :], bank(j % 2)[0:w, :], ACT.Silu).then_inc(S["silu_done"], 1)
                else:
                    for t in range(TT):
                        act.wait_ge(S["hl_ready"], t + 1)
                        act.activation(hl[:, t, :], bank(t % 2)[:, 0:E * R + E], ACT.Copy).then_inc(S["hl_sb"], 1)
                    act.wait_ge(S["gap_done"], 1)
                    act.activation(egap, gap, ACT.Exp).then_inc(S["egap_done"], 1)
                    for t in range(TT):
                        act.wait_ge(S["hwT_ready"], t + 1)
                        act.activation(hwT[:, t, :], bank(2 + t % 2)[:, 0:P], ACT.Copy).then_inc(S["hwT_sb"], 1)
                if l == 0:
                    act.wait_ge(S["wp_in"], 16 * 8)
                for c in range(NCH):
                    if c:
                        act.wait_ge(S["rest_ready"], c * NQ)
                    for m in range(NQ):
                        rows = DH if (m == KC and l == 0) else P
                        bias = 0.0 if l else (bias_q[:, m:m + 1] if m < KC else bias_k[:, 0:1])
                        act.wait_ge(S["q_ready"], c * NQ + m + 1)
                        act.activation(q32[m][0:rows, :], bank(m)[0:rows, :], ACT.Identity, bias=bias).then_inc(S["q32_ready"], 1)

                items = [main_items(l == 1, c) for c in range(QC)]
                group_items = per_group[l]
                for m in range(NQ):
                    act.wait_ge(S["q_out"][m], 16 * PARTS * NCH)
                for c in range(QC):
                    act.sem_inc(S["o_out"][c], 16)
                act.sem_inc(S["p_ready"], SP_RING)

                def attend(it):
                    base = it * (SLOTS * group_items)
                    local = 0

                    def copy_o(u, c, through):
                        n = it * SLOTS + u
                        act.wait_ge(S["pv_done"], base + through + P_RING)
                        act.wait_ge(S["o_out"][c], n * 80 + 16)
                        act.activation(o_sb[c], bank(7), ACT.Copy).then_inc(S["o_copied"], 1)

                    before = None
                    for u in range(SLOTS):
                        for c in range(QC):
                            for i, (kt, h, q0) in enumerate(items[c]):
                                act.wait_ge(S["s_ready"], base + local + 1)
                                act.wait_ge(S["pv_done"], base + local + 1)
                                act.activation(prob[local % P_RING][:, q0:CH], bank(local % SP_RING)[:, q0:CH],
                                               ACT.Exp, scale=SCALE).then_inc(S["p_ready"], 1)
                                local += 1
                                if i == 1 and before:
                                    copy_o(*before)
                            before = (u, c, local)
                    copy_o(*before)

                with act.Fori(0, ITERS - 1) as it:
                    attend(it)
                attend(ITERS - 1)

        @block.vector
        def _(dve):
            made = [0]
            dve.wait_ge(x_in, 16)
            for l in (0, 1):
                S = L[l]
                for t in range(TT):
                    dve.bn_stats(stats[:, t, :], acc[:, t, :]).then_inc(dve_chain, 1)
                    made[0] += 1
                dve.wait_ge(dve_chain, made[0])
                for t in range(TT):
                    dve.bn_aggr(mv[:, t, :], stats[:, t, :]).then_inc(dve_chain, 1)
                    made[0] += 1
                dve.wait_ge(dve_chain, made[0])
                dve.tensor_scalar(var[:, :], mv[:, :, 1], EPS, None, ALU.add).then_inc(S["eps_done"], 1)
                dve.wait_ge(S["sqrt_done"], 1)
                dve.reciprocal(rstd[:, :], std[:, :]).then_inc(dve_chain, 1)
                made[0] += 1
                dve.wait_ge(dve_chain, made[0])
                dve.tensor_tensor(nwt[:, :], rstd[:, :], rstd[:, :], ALU.mult).then_inc(dve_chain, 1)
                made[0] += 1
                dve.wait_ge(dve_chain, made[0])
                dve.tensor_tensor(std[:, :], nwt[:, :], var[:, :], ALU.mult).then_inc(dve_chain, 1)
                made[0] += 1
                dve.wait_ge(dve_chain, made[0])
                dve.tensor_scalar(nwt[:, :], std[:, :], -0.5, 1.5, ALU.mult, ALU.add).then_inc(dve_chain, 1)
                made[0] += 1
                dve.wait_ge(dve_chain, made[0])
                dve.tensor_tensor(std[:, :], rstd[:, :], nwt[:, :], ALU.mult).then_inc(dve_chain, 1)
                made[0] += 1
                dve.wait_ge(dve_chain, made[0])
                for t in range(TT):
                    if t >= 2:
                        dve.wait_ge(S["xn_T"], t - 1)
                    dve.tensor_scalar(xn[t % 2], acc[:, t, :], mv[:, t, 0:1], std[:, t:t + 1], ALU.subtract, ALU.mult).then_inc(S["xn_ready"], 1)
                dve.wait_ge(S["acc_biased"], TT)
                if l == 0:
                    with dve.Fori(0, NCH) as c:
                        for j in range(FT):
                            w = width_f(j)
                            dve.wait_ge(S["silu_done"], c * FT + j + 1)
                            dve.tensor_tensor(hid[j % 2][0:w, :], sil[j % 2][0:w, :], bank(2 + j % 2)[0:w, :], ALU.mult).then_inc(S["hid_done"], 1)
                        for t in range(TPC):
                            dve.wait_ge(S["y_ready"], c * TPC + t + 1)
                            a = acc[:, bass.ds(c * TPC + t, 1), :].rearrange("p o d -> p (o d)")
                            dve.tensor_tensor(a, a, bank(4 + t), ALU.add).then_inc(S["y_evac"], 1)
                else:
                    dve.wait_ge(iota_done, 2)
                    dve.wait_ge(S["hl_sb"], TT)
                    lg = hl[:, :, E * R:E * R + E]
                    for t in range(TT):
                        dve.max(top[:, t, :], lg[:, t, :]).then_inc(dve_chain, 1)
                        made[0] += 1
                    dve.wait_ge(dve_chain, made[0])
                    dve.tensor_tensor(gap, top[:, :, 1], top[:, :, 0], ALU.subtract).then_inc(S["gap_done"], 1)
                    for t in range(TT):
                        dve.max_index(topi[:, t, :], top[:, t, :], lg[:, t, :]).then_inc(dve_chain, 1)
                        made[0] += 1
                    dve.wait_ge(dve_chain, made[0])
                    dve.tensor_copy(topf, topi[:, :, 0:2]).then_inc(dve_chain, 1)
                    made[0] += 1
                    dve.wait_ge(S["egap_done"], 1)
                    dve.tensor_scalar(esum, egap, 1.0, None, ALU.add).then_inc(dve_chain, 1)
                    made[0] += 1
                    dve.wait_ge(dve_chain, made[0])
                    dve.reciprocal(winv, esum).then_inc(dve_chain, 1)
                    made[0] += 1
                    dve.wait_ge(dve_chain, made[0])
                    dve.tensor_scalar(wt1, winv, 2.0, None, ALU.mult).then_inc(dve_chain, 1)
                    made[0] += 1
                    dve.wait_ge(dve_chain, made[0])
                    dve.tensor_tensor(wt2, wt1, egap, ALU.mult).then_inc(dve_chain, 1)
                    made[0] += 1
                    dve.wait_ge(dve_chain, made[0])
                    dve.wait_ge(dve_chain, made[0])
                    for t in range(TT):
                        dve.tensor_scalar(gate1[:, t, :], iota8, topf[:, t, 0:1], wt1[:, t:t + 1], ALU.is_equal, ALU.mult).then_inc(dve_chain, 1)
                        made[0] += 1
                        dve.tensor_scalar(gate2[:, t, :], iota8, topf[:, t, 1:2], wt2[:, t:t + 1], ALU.is_equal, ALU.mult).then_inc(dve_chain, 1)
                        made[0] += 1
                    dve.wait_ge(dve_chain, made[0])
                    dve.tensor_tensor(gate, gate1, gate2, ALU.add).then_inc(dve_chain, 1)
                    made[0] += 1
                    dve.wait_ge(dve_chain, made[0])
                    for t in range(TT):
                        g = gate[:, t, :].rearrange("p (e o) -> p e o", o=1).to_broadcast([P, E, R])
                        dve.tensor_tensor(hw[:, t, :].rearrange("p (e r) -> p e r", e=E),
                                          hl[:, t, 0:E * R].rearrange("p (e r) -> p e r", e=E), g, ALU.mult).then_inc(S["hw_done"], 1)
                    for t in range(TT):
                        dve.wait_ge(S["b_ready"], t + 1)
                        dve.tensor_tensor(acc[:, t, :], acc[:, t, :], bank(4 + t % 4), ALU.add).then_inc(S["b_evac"], 1)

                if l:
                    dve.wait_ge(rope_in, 32)
                for c in range(NCH):
                    pos = slice(c % QC * CH, (c % QC + 1) * CH)
                    for m in range(NQ):
                        rows = DH if (m == KC and l == 0) else P
                        dve.wait_ge(S["q32_ready"], c * NQ + m + 1)
                        if c:
                            dve.wait_ge(S["q_out"][m], c * (16 * PARTS))
                        if l:
                            dve.stream_shuffle(rest[m], q32[m], swap).then_inc(dve_chain, 1)
                            made[0] += 1
                            dve.wait_ge(dve_chain, made[0])
                            dve.tensor_tensor(q32[m], q32[m], rope_cos[:, pos], ALU.mult).then_inc(dve_chain, 1)
                            dve.tensor_tensor(rest[m], rest[m], rope_sin[:, pos], ALU.mult).then_inc(dve_chain, 1)
                            made[0] += 2
                            dve.wait_ge(dve_chain, made[0])
                            dve.tensor_tensor(q32[m], q32[m], rest[m], ALU.add).then_inc(dve_chain, 1)
                            made[0] += 1
                            dve.wait_ge(dve_chain, made[0])
                        dve.tensor_copy(part[m][0:rows, 0, :], q32[m][0:rows, :]).then_inc(S["hi_done"], 1)
                        dve.wait_ge(S["hi_done"], c * NQ + m + 1)
                        dve.tensor_tensor(rest[m][0:rows, :], q32[m][0:rows, :], part[m][0:rows, 0, :], ALU.subtract).then_inc(S["rest_ready"], 1)
                for t in range(TT):
                    b, kt = divmod(t, KT)
                    kv = (1, NG)[l]
                    dve.wait_ge(S["v_ready"], t + 1)
                    dst = v_all[:, b * kv:(b + 1) * kv, kt, 0:DH]
                    src = bank(5 + t % 3)[:, 0:KVW[l]].rearrange("p (h d) -> p h d", h=kv)
                    if l == 0:
                        dve.tensor_tensor(dst, src, bias_v[:, :].rearrange("p (h d) -> p h d", h=1), ALU.add).then_inc(S["v_done"], 1)
                    else:
                        dve.tensor_copy(dst, src).then_inc(S["v_done"], 1)

                for m in range(NQ):
                    dve.wait_ge(S["q_out"][m], 16 * PARTS * NCH)

                def maxima(n):
                    jx = n * (QC * XI)
                    for c in range(QC):
                        for qt in range(TPC):
                            for h in range(HG):
                                w = max_width(l == 1, c, qt)
                                dve.wait_ge(S["x_ready"], jx + 1)
                                dve.tensor_reduce(maxes[c][:, h * TPC + qt:h * TPC + qt + 1], bank(3 + 2 * jpar[0], 2)[:, 0:w],
                                                  AX_X, ALU.max).then_inc(S["x_done"], 1)
                                jx = jx + 1
                                jpar[0] ^= 1
                        dve.wait_ge(S["x_ready"], jx + 1)
                        if not (isinstance(n, int) and n == 0):
                            dve.wait_ge(S["m_in"][c], n * (16 * MROWS))
                        mt = bank(3 + 2 * jpar[0])[0:NX, 0:P]
                        dve.tensor_scalar(negm[c][0:NX, 0, :], mt, -1.0, None, ALU.mult).then_inc(S["mhi_done"], 1)
                        dve.wait_ge(S["mhi_done"], n * QC + c + 1)
                        last = dve.scalar_tensor_tensor(negm[c][0:NX, 1, :], mt, -1.0, negm[c][0:NX, 0, :], ALU.mult, ALU.subtract)
                        last.then_inc(S["m_ready"], 1)
                        dve.wait_ge(S["m_ready"], n * QC + c + 1)
                        dve.sem_inc(S["x_done"], 1)
                        jx = jx + 1
                        jpar[0] ^= 1

                jpar = [0]
                maxima(0)
                with dve.Fori(1, B * NG) as n:
                    maxima(n)

                for i in range(B * KC):
                    b, t = divmod(i, KC)
                    dve.wait_ge(S["num_in"][i], 16 * (1 + P // DH))
                    dve.reciprocal(den[i % 2], den[i % 2]).then_inc(S["den_inv"], 1)
                    dve.wait_ge(S["den_inv"], i + 1)
                    a = xnT[:, t, b * N:(b + 1) * N]
                    dve.tensor_tensor(a, a, den[i % 2], ALU.mult).then_inc(S["on_ready"], 1)
                for t in range(TT):
                    dve.wait_ge(S["y2_ready"], t + 1)
                    if l == 0:
                        dve.tensor_tensor(acc[:, t, :], acc[:, t, :], bank(t % 8), ALU.add).then_inc(S["y2_evac"], 1)
                    else:
                        if t >= 4:
                            dve.wait_ge(S["stored"][t % 4], 16 * (t // 4))
                        dve.tensor_tensor(res[t % 4], acc[:, t, :], bank(t % 8), ALU.add).then_inc(S["y2_evac"], 1)
                if l == 0:
                    dve.wait_ge(S["y2_evac"], TT)

        @block.tensor
        def _(pe):
            pe.wait_ge(const_b, 4)
            for l in (0, 1):
                S = L[l]
                pe.sem_inc(S["xnT_ready"], 1)
                with pe.Fori(0, TT // 2) as i:
                    for j in range(2):
                        pe.wait_ge(S["xn_ready"], i * 2 + j + 1)
                        pe.wait_ge(S["xnT_ready"], i * 2 + 1)
                        for k in range(KC):
                            last = pe.transpose(bank(j)[:, k * P:(k + 1) * P], xn[j][:, k * P:(k + 1) * P], ident[:, :])
                        last.then_inc(S["xn_T"], 1)
                pe.wait_ge(S["xnT_ready"], TT + 1)
                if l == 0:
                    pe.wait_ge(S["wf_in"], 16 * 3)
                    pe.sem_inc(S["hid_done"], 1)
                    pe.sem_inc(S["y_evac"], 1)
                    with pe.Fori(0, NCH) as c:
                        def down(j):
                            w = width_f(j)
                            pe.wait_ge(S["hid_done"], c * FT + j + 2)
                            if j == 0:
                                pe.wait_ge(S["y_evac"], c * TPC + 1)
                            for t in range(TPC):
                                last = pe.matmul(bank(4 + t), hid[j % 2][0:w, t * P:(t + 1) * P], w_dn[0:w, j, :],
                                                 start=(j == 0), stop=(j == FT - 1))
                                if j == FT - 1:
                                    last.then_inc(S["y_ready"], 1)

                        for j in range(FT):
                            w = width_f(j)
                            pe.wait_ge(S["hid_done"], c * FT + max(1, j))
                            for half in range(2):
                                for k in range(KC):
                                    f0 = half * F + j * P
                                    last = pe.matmul(bank(2 * half + j % 2)[0:w, :], w_gu[:, k, f0:f0 + w],
                                                     xnT[:, k, bass.ts(c, CH)], start=(k == 0), stop=(k == KC - 1))
                            last.then_inc(S["gu_ready"], 1)
                            if j >= 1:
                                down(j - 1)
                        down(FT - 1)
                else:
                    pe.wait_ge(S["wf_in"], 16 * 4)
                    for t in range(TT):
                        if t >= 2:
                            pe.wait_ge(S["hl_sb"], t - 1)
                        for k in range(KC):
                            last = pe.matmul(bank(t % 2)[:, 0:E * R + E], xnT[:, k, t * P:(t + 1) * P], w_ar[:, k, :],
                                             start=(k == 0), stop=(k == KC - 1))
                        last.then_inc(S["hl_ready"], 1)
                    for t in range(TT):
                        pe.wait_ge(S["hw_done"], t + 1)
                        if t >= 2:
                            pe.wait_ge(S["hwT_sb"], t - 1)
                        pe.transpose(bank(2 + t % 2)[:, 0:P], hw[:, t, :], ident[:, :]).then_inc(S["hwT_ready"], 1)
                    for t in range(TT):
                        if t >= 4:
                            pe.wait_ge(S["b_evac"], t - 3)
                        for k in range(KC):
                            pe.matmul(bank(4 + t % 4), xnT[:, k, t * P:(t + 1) * P], w_base[:, k, :], start=(k == 0), stop=False)
                        pe.wait_ge(S["hwT_sb"], t + 1)
                        pe.matmul(bank(4 + t % 4), hwT[:, t, :], w_lb, start=False, stop=True).then_inc(S["b_ready"], 1)

                pe.wait_ge(S["wp_in"], 16 * (8 if l == 0 else 5))
                if l == 0:
                    pe.wait_ge(S["y_evac"], TT + 1)
                else:
                    pe.wait_ge(S["b_evac"], TT)
                kw = KVW[l]
                for c in range(NCH):
                    if c:
                        pe.wait_ge(S["q32_ready"], c * NQ)
                    for m in range(NQ):
                        for k in range(KC):
                            w = w_q[:, k, m * P:(m + 1) * P] if m < KC else w_kv[:, k, 0:kw]
                            last = pe.matmul(bank(m) if m < KC else bank(m)[0:kw, :], w, xnT[:, k, c * CH:(c + 1) * CH],
                                             start=(k == 0), stop=(k == KC - 1))
                        last.then_inc(S["q_ready"], 1)
                for t in range(TT):
                    if t >= 3:
                        pe.wait_ge(S["v_done"], t - 2)
                    for k in range(KC):
                        last = pe.matmul(bank(5 + t % 3)[:, 0:kw], xnT[:, k, t * P:(t + 1) * P], w_kv[:, k, kw:2 * kw],
                                         start=(k == 0), stop=(k == KC - 1))
                    last.then_inc(S["v_ready"], 1)
                pe.wait_ge(S["v_done"], TT)
                pe.wait_ge(S["q32_ready"], NCH * NQ)

                causal = l == 1
                items = [main_items(causal, c) for c in range(QC)]
                group_items = per_group[l]
                pe.sem_inc(S["o_copied"], 1)
                pe.sem_inc(S["pv_done"], P_RING)

                def max_items():
                    r = []
                    for c in range(QC):
                        r += [(c, qt, h) for qt in range(TPC) for h in range(HG)] + [(c, None, None)]
                    return r

                XL = max_items()

                def max_item(n, u, e):
                    c, qt, h = XL[e]
                    dst = bank(3 + 2 * (e % 2), 2)
                    j = n * len(XL) + e
                    if not (isinstance(j, int) and j < 2):
                        pe.wait_ge(S["x_done"], j - 1)
                    if qt is None:
                        pe.wait_ge(S["x_done"], j)
                        pe.transpose(dst[0:NX, 0:P], maxes[c], ident[:, :]).then_inc(S["x_ready"], 1)
                        return
                    w = max_width(causal, c, qt)
                    lhs = q_slot[u][0:ROWS, c, h, qt * P:(qt + 1) * P]
                    for k0 in range(0, w, CH):
                        k1 = min(w, k0 + CH)
                        diag = causal and k1 == w
                        last = pe.matmul(dst[:, k0:k1], lhs, k_slot[u][0:ROWS, k0:k1], start=True, stop=not diag)
                        if diag:
                            last = pe.matmul(dst[:, w - P:w], identb[:, :], mask_qk[:, :], start=False, stop=True)
                    last.then_inc(S["x_ready"], 1)

                def attend(it, last_iter):
                    base = it * (SLOTS * group_items)
                    pending = []
                    local = 0

                    def pv():
                        idx, u, c, kt, h, q0, nkt = pending.pop(0)
                        pe.wait_ge(S["p_ready"], base + idx + 1 + SP_RING)
                        if kt == 0 and h == 0:
                            pe.wait_ge(S["o_copied"], (it * SLOTS + u) * QC + c + 1)
                        mm = pe.matmul(bank(7)[32 * h:32 * h + DH + 1, q0:CH], v_slot[u][:, kt, :], prob[idx % P_RING][:, q0:CH],
                                       start=(kt == 0), stop=(kt == nkt - 1), tile_position=(0, 32 * h))
                        mm.then_inc(S["pv_done"], 1)

                    for u in range(SLOTS):
                        n = it * SLOTS + u
                        has_next = not (last_iter and u == SLOTS - 1)
                        v = (u + 1) % SLOTS
                        if has_next:
                            itv = it if u + 1 < SLOTS else it + 1
                            pe.wait_ge(S["slot_in"][v], (itv + 1) * (16 * 12))
                        pe.wait_ge(S["v_slot_ready"], n + 1 + SLOTS)
                        done = 0
                        i_g = 0
                        for c in range(QC):
                            nkt = len(items[c]) // HG
                            for i, (kt, h, q0) in enumerate(items[c]):
                                if i == 0:
                                    pe.wait_ge(S["m_in"][c], (n + 1) * (16 * MROWS))
                                slot = local % SP_RING
                                free = local if local >= SP_RING else first_free[local]
                                pe.wait_ge(S["p_ready"], base + free + 1)
                                diag = causal and kt >= TPC * c
                                mm = pe.matmul(bank(slot)[:, q0:CH], k_slot[u][0:ROWS + MROWS, kt * P:(kt + 1) * P],
                                               q_slot[u][0:ROWS + MROWS, c, h, q0:CH], start=True, stop=not diag)
                                if diag:
                                    mm = pe.matmul(bank(slot)[:, q0:q0 + P], identb[:, :], mask_kq[:, :], start=False, stop=True)
                                mm.then_inc(S["s_ready"], 1)
                                pending.append((local, u, c, kt, h, q0, nkt))
                                local += 1
                                i_g += 1
                                if has_next:
                                    while done < (i_g * len(XL)) // group_items:
                                        max_item(n + 1, v, done)
                                        done += 1
                                if len(pending) > LAG:
                                    pv()
                    while pending:
                        pv()

                total = SLOTS * group_items
                first_free = []
                for s in range(SP_RING):
                    lastuse = max(i for i in range(total) if i % SP_RING == s) - total
                    first_free.append(lastuse + SP_RING)

                pe.wait_ge(S["slot_in"][0], 16 * 12)
                pe.wait_ge(S["v_slot_ready"], SLOTS)
                for e in range(len(XL)):
                    max_item(0, 0, e)
                with pe.Fori(0, ITERS - 1) as it:
                    attend(it, False)
                attend(ITERS - 1, True)

                pe.wait_ge(S["o_copied"], B * NG * QC + 1)
                for t in range(TT):
                    pe.wait_ge(S["on_ready"], KC if t < KT else 2 * KC)
                    if t >= 8:
                        pe.wait_ge(S["y2_evac"], t - 7)
                    for k in range(KC):
                        last = pe.matmul(bank(t % 8), xnT[:, k, t * P:(t + 1) * P], w_o[:, k, :], start=(k == 0), stop=(k == KC - 1))
                    last.then_inc(S["y2_ready"], 1)
                pe.wait_ge(S["y2_evac"], TT)


def kernel(**inputs):
    import numpy as _np
    import concourse.bacc as _bacc
    from concourse import mybir as _mybir
    from concourse.bass_utils import run_bass_kernel_spmd as _run

    def flat(name):
        return _np.ascontiguousarray(inputs[name])

    lb = flat("L1_ffn_lora_B")
    laid = {
        "x": flat("L0_attn_x").reshape(T, D),
        "wq0": flat("L0_attn_Wq"), "bq0": _np.ascontiguousarray(flat("L0_attn_bq").reshape(KC, P).T), "wk0": flat("L0_attn_Wk"), "bk0": flat("L0_attn_bk"),
        "wv0": flat("L0_attn_Wv"), "bv0": flat("L0_attn_bv"), "wo0": flat("L0_attn_Wo"), "bo0": flat("L0_attn_bo"),
        "wgu": _np.ascontiguousarray(flat("L0_ffn_w_gate_up").T), "wdn": _np.ascontiguousarray(flat("L0_ffn_w_down").T),
        "wq1": flat("L1_attn_Wq"), "wk1": flat("L1_attn_Wk"), "wv1": flat("L1_attn_Wv"), "wo1": flat("L1_attn_Wo"),
        "wbase": _np.ascontiguousarray(flat("L1_ffn_W_base").T), "bbase": flat("L1_ffn_b_base"),
        "wrt": _np.ascontiguousarray(flat("L1_ffn_W_router").T),
        "la": _np.ascontiguousarray(flat("L1_ffn_lora_A").reshape(E * R, D).T),
        "lb": _np.ascontiguousarray(lb.transpose(0, 2, 1)).reshape(E * R, D),
    }
    freq = (_np.float32(1.0) / _np.float32(10000.0) ** (_np.arange(0, DH, 2, dtype=_np.float32) / _np.float32(DH))).astype(_np.float32)
    angle = (_np.arange(N, dtype=_np.float32)[None, :] * _np.tile(_np.repeat(freq, 2), P // DH)[:, None]).astype(_np.float32)
    sign = _np.where(_np.arange(P) % 2 == 0, -1.0, 1.0).astype(_np.float32)
    laid["rcos"] = _np.cos(angle).astype(_np.float32)
    laid["rsin"] = (_np.sin(angle) * sign[:, None]).astype(_np.float32)
    nc = _bacc.Bacc("TRN2", target_bir_lowering=False, num_devices=1)
    arrays, args = {}, []
    for name, a in laid.items():
        arrays[f"in_{name}"] = a
        args.append(nc.dram_tensor(f"in_{name}", a.shape, _mybir.dt.from_np(a.dtype), kind="ExternalInput").ap())
    args.append(nc.dram_tensor("out_0", (T, D), F32, kind="ExternalOutput").ap())
    build(nc, *args)
    r = _run(nc, [arrays], core_ids=[0])
    return r.results[0]["out_0"].reshape(B, N, D)
```

```python
from contextlib import ExitStack

import concourse.bass as bass
from concourse import mybir

ALU = mybir.AluOpType
ACT = mybir.ActivationFunctionType
BF16 = mybir.dt.bfloat16
F32 = mybir.dt.float32
F32R = mybir.dt.float32r
U32 = mybir.dt.uint32
AX_X = mybir.AxisListType.X

P = 128
B, N, D = 2, 1024, 512
T = B * N
TT = T // P
KC = D // P
CH = 512
NCH = T // CH
H, DH = 32, 16
HG = 4
NG = H // HG
KT = N // P
QC = N // CH
TPC = CH // P
F = 1376
FT = -(-F // P)
E, R = 8, 16
W_SLOTS = 3
ROUNDS = [list(range(j, min(j + W_SLOTS, FT))) for j in range(0, FT, W_SLOTS)]
EPS = 1e-5
SCALE = 1.0 / DH ** 0.5
MASKED = -1e30
SLOTS = 4
ITERS = B * NG // SLOTS
SP_RING, P_RING, LAG = 3, 8, 3
PARTS = 3
ROWS = 6 * DH
MROWS = 2
XN_RING = 8
NX = TPC * HG
XI = NX + 1


def width_f(j):
    return min(P, F - j * P)


def main_items(causal, qc):
    kts = TPC * (qc + 1) if causal else KT
    return [(kt, h, max(0, kt - TPC * qc) * P if causal else 0) for kt in range(kts) for h in range(HG)]


def weight_views(t, j):
    w = width_f(j)
    gu = KC * 2 * P
    return (t[:, 0:gu].rearrange("p (q c) -> p q c", c=P)[:, :, 0:w], t[0:w, gu:gu + D])


def max_items():
    r = [[(c, qt, h) for qt in range(TPC) for h in range(HG)] for c in range(QC)]
    return r[0] + r[1][:2] + [(0, None, None)] + r[1][2:] + [(1, None, None)]


def max_width(causal, qc, qt):
    return (TPC * qc + qt + 1) * P if causal else N


def build(nc, x, wq0, bq0, wk0, bk0, wv0, bv0, wo0, bo0, wgu, wdn, wq1, wk1, wv1, wo1,
          wbase, bbase, wrt, la, lb, rcos, rsin, out):
    ctx = ExitStack()
    with ctx:
        def sb(name, shape, dt=F32):
            return ctx.enter_context(nc.sbuf_tensor(name, shape, dt))

        def sem(name):
            return ctx.enter_context(nc.semaphore(name))

        qparts = [nc.dram_tensor(f"qparts{l}", [B * H, PARTS * DH, N], BF16, kind="Internal").ap() for l in (0, 1)]
        kparts = [nc.dram_tensor(f"kparts{l}", [B * kv, PARTS * DH, N], BF16, kind="Internal").ap()
                  for l, kv in ((0, 1), (1, NG))]
        numer = [nc.dram_tensor(f"numer{l}", [B * H, DH, N], F32, kind="Internal").ap() for l in (0, 1)]
        inverse = [nc.dram_tensor(f"inverse{l}", [B * H, N], F32, kind="Internal").ap() for l in (0, 1)]
        denom = [nc.dram_tensor(f"denom{l}", [B * H, N], F32, kind="Internal").ap() for l in (0, 1)]

        acc = sb("acc", [P, TT, D])
        xnT = sb("xnT", [P, KC, T])
        w_q = sb("w_q", [P, KC, D])
        w_kv = sb("w_kv", [P, KC, 256])
        w_o = sb("w_o", [P, KC, D])
        bias_q = sb("bias_q", [P, KC])
        bias_k = sb("bias_k", [DH, 1])
        bias_v = sb("bias_v", [P, DH])
        bias_o = sb("bias_o", [P, D])
        v_all = sb("v_all", [P, B * NG, KT, DH + 1])
        ident = sb("ident", [P, P])
        identb = sb("identb", [P, P], BF16)
        mask_kq = sb("mask_kq", [P, P], BF16)
        mask_qk = sb("mask_qk", [P, P], BF16)
        stats = sb("stats", [P, TT, 6])
        mv = sb("mv", [P, TT, 2])
        var = sb("var", [P, TT])
        std = sb("std", [P, TT])
        rstd = sb("rstd", [P, TT])
        nwt = sb("nwt", [P, TT])
        with ExitStack() as own:
            def fb(name, shape, dt=F32):
                return own.enter_context(nc.sbuf_tensor(name, shape, dt))

            GU = KC * 2 * P
            w_hi = fb("w_hi", [P, W_SLOTS, GU + D], F32R)
            w_lo = fb("w_lo", [P, W_SLOTS, GU + D], F32R)
            x_hi = fb("x_hi", [P, 2, KC, CH], F32R)
            x_lo = fb("x_lo", [P, 2, KC, CH], F32R)
            h_hi = fb("h_hi", [P, 2, CH], F32R)
            h_lo = fb("h_lo", [P, 2, CH], F32R)
            w_raw = fb("w_raw", [P, 2, GU + D])
            xn0 = fb("xn0", [P, XN_RING, D])
            sil = xn0[:, 0:2, :]
            hid = xn0[:, 2:4, :]
        AR = 25 * 1024
        arena = sb("arena", [P, AR])

        used = [0]

        def region(cols, dt=F32, parts=P):
            a = used[0]
            used[0] += cols
            assert used[0] <= AR, used[0]
            v = arena[0:parts, a:a + cols]
            return v if dt == F32 else v.bitcast(dt)

        xn = [[xn0[:, i, :] for i in range(XN_RING)], [region(D) for _ in range(XN_RING)]]
        used[0] = XN_RING * D
        w_base = region(KC * D).rearrange("p (k f) -> p k f", k=KC)
        w_ar = region(KC * (E * R + E)).rearrange("p (k f) -> p k f", k=KC)
        w_lb = region(D)
        hl = region(TT * (E * R + E)).rearrange("p (t f) -> p t f", t=TT)
        hw = region(TT * E * R).rearrange("p (t f) -> p t f", t=TT)
        hwT = region(TT * P).rearrange("p (t f) -> p t f", t=TT)
        top = region(TT * 8).rearrange("p (t f) -> p t f", t=TT)
        topi = region(TT * 8, U32).rearrange("p (t f) -> p t f", t=TT)
        topf = region(TT * 2).rearrange("p (t f) -> p t f", t=TT)
        gap = region(TT)
        egap = region(TT)
        esum = region(TT)
        winv = region(TT)
        wt1 = region(TT)
        wt2 = region(TT)
        gate1 = region(TT * E).rearrange("p (t f) -> p t f", t=TT)
        gate2 = region(TT * E).rearrange("p (t f) -> p t f", t=TT)
        gate = region(TT * E).rearrange("p (t f) -> p t f", t=TT)
        iota8 = region(E)
        NQ = KC + 1
        used[0] = 0
        q32 = [region(CH) for _ in range(NQ)]
        rest = [region(CH) for _ in range(NQ)]
        part = [region(PARTS * CH // 2, BF16).rearrange("p (s q) -> p s q", s=PARTS) for _ in range(NQ)]
        rope_cos = region(N)
        rope_sin = region(N)
        used[0] = 0
        q_slot = [region(HG * N // 2, BF16).rearrange("p (c h q) -> p c h q", c=QC, h=HG) for _ in range(SLOTS)]
        k_slot = [region(N // 2, BF16) for _ in range(SLOTS)]
        v_slot = [region(KT * (DH + 1)).rearrange("p (k d) -> p k d", k=KT) for _ in range(SLOTS)]
        prob = [region(CH) for _ in range(P_RING)]
        o_sb = [region(CH) for _ in range(QC)]
        maxes = [region(NX) for _ in range(QC)]
        negm = [region(MROWS * P // 2, BF16).rearrange("p (s q) -> p s q", s=MROWS) for _ in range(QC)]
        inv = [region(H * N // P) for _ in range(B)]
        den = [[region(N) for _ in range(KC)] for _ in range(B)]
        res = [den[0][i][:, 0:D] for i in range(4)]

        ps = ctx.enter_context(nc.psum_tensor("ps", [P, 8 * CH], F32))

        def bank(i, n=1):
            return ps[:, i * CH:(i + n) * CH]

        def sems(l):
            names = (
                     "eps_done sqrt_done xn_ready xn_T xnT_ready acc_biased q_ready q32_ready hi_done rest_ready "
                     "mid_done lo_done v_ready v_done v_slot_ready s_ready p_ready pv_done o_copied x_ready "
                     "x_done mhi_done m_ready inv_ready on_ready0 on_ready1 y2_ready y2_evac ").split()
            names += ((
                     "gu_ready silu_done prod_done hhi_done hid_done whi_done w_ready xhi_done xc_ready y_ready "
                     "y_evac ").split(), (
                     "hl_ready hl_sb gap_done egap_done hw_done hwT_ready hwT_sb b_ready b_evac ").split())[l]
            S = {n: sem(f"{n}_{l}") for n in names}
            S["q_out"] = [sem(f"q_out{m}_{l}") for m in range(NQ)]
            S["slot_in"] = [sem(f"slot_in{u}_{l}") for u in range(SLOTS)]
            S["m_in"] = [sem(f"m_in{c}_{l}") for c in range(QC)]
            S["o_out"] = [sem(f"o_out{c}_{l}") for c in range(QC)]
            S["den_in"] = [sem(f"den_in{b}_{l}") for b in range(B)]
            S["inv_out"] = [sem(f"inv_out{b}_{l}") for b in range(B)]
            S["num_in"] = [sem(f"num_in{i}_{l}") for i in range(B * KC)]
            S["raw_in"] = [sem(f"raw_in{i}_{l}") for i in range(2 - 2 * l)]
            S["stored"] = [sem(f"stored{i}_{l}") for i in range(4 * l)]
            S["wf_in"] = sem(f"wf_in_{l}")
            S["wp_in"] = sem(f"wp_in_{l}")
            return S

        L = [sems(0), sems(1)]
        x_in = [sem(f"x_in{g}") for g in range(NCH)]
        rope_in = sem("rope_in")
        swap = [i ^ 1 for i in range(32)]
        const_a = sem("const_a")
        const_b = sem("const_b")
        iota_done = sem("iota_done")
        dve_chain = sem("dve_chain")

        KVW = [DH, NG * DH]
        per_group = [sum(len(main_items(l == 1, c)) for c in range(QC)) for l in (0, 1)]

        block = ctx.enter_context(nc.Block())

        @block.sync
        def _(sp):
            for g in range(NCH):
                sp.dma_start(acc[:, g * TPC:(g + 1) * TPC, :],
                             x[g * CH:(g + 1) * CH, :].rearrange("(t p) d -> p t d", p=P)).then_inc(x_in[g], 16)

            def load_projections(l):
                S = L[l]
                wq, wk, wv, wo = ((wq0, wk0, wv0, wo0), (wq1, wk1, wv1, wo1))[l]
                kw = KVW[l]
                r = "(k p) n -> p k n"
                sp.dma_start(w_q[:, :, :], wq.rearrange(r, p=P)).then_inc(S["wp_in"], 16)
                sp.dma_start(w_kv[:, :, 0:kw], wk.rearrange(r, p=P)).then_inc(S["wp_in"], 16)
                sp.dma_start(w_kv[:, :, kw:2 * kw], wv.rearrange(r, p=P)).then_inc(S["wp_in"], 16)
                sp.dma_start(w_o[:, :, :], wo.rearrange(r, p=P)).then_inc(S["wp_in"], 16)
                if l == 0:
                    sp.dma_start(bias_q[:, :], bq0).then_inc(S["wp_in"], 16)
                    sp.dma_start(bias_k[:, :], bk0.rearrange("(p a) -> p a", a=1)).then_inc(S["wp_in"], 16)
                    sp.dma_start(bias_v[:, :], bv0.partition_broadcast(P)).then_inc(S["wp_in"], 16)
                    sp.dma_start(bias_o[:, :], bo0.partition_broadcast(P)).then_inc(S["wp_in"], 16)
                else:
                    sp.dma_start(bias_o[:, :], bbase.partition_broadcast(P)).then_inc(S["wp_in"], 16)

            def load_ffn0(js):
                S = L[0]
                for j in js:
                    w = width_f(j)
                    raw = w_raw[:, j % 2, :]
                    gu = raw[:, 0:GU].rearrange("p (k g c) -> p k g c", k=KC, g=2)
                    if j >= 2:
                        sp.wait_ge(S["w_ready"], j - 1)
                    for g in range(2):
                        sp.dma_start(gu[:, :, g, 0:w], wgu[:, g * F + j * P:g * F + j * P + w].rearrange("(k p) n -> p k n", p=P)).then_inc(S["raw_in"][j % 2], 16)
                    sp.dma_start(raw[0:w, GU:GU + D], wdn[j * P:j * P + w, :]).then_inc(S["raw_in"][j % 2], 16)

            def load_ffn1():
                S = L[1]
                r = "(k p) n -> p k n"
                sp.dma_start(w_base, wbase.rearrange(r, p=P)).then_inc(S["wf_in"], 16)
                sp.dma_start(w_ar[:, :, 0:E * R], la.rearrange(r, p=P)).then_inc(S["wf_in"], 16)
                sp.dma_start(w_ar[:, :, E * R:E * R + E], wrt.rearrange(r, p=P)).then_inc(S["wf_in"], 16)
                sp.dma_start(w_lb, lb).then_inc(S["wf_in"], 16)

            def store_parts(l):
                S = L[l]
                with sp.Fori(0, B) as b:
                    with sp.Fori(0, QC) as cc:
                        for m in range(NQ):
                            sp.wait_ge(S["lo_done"], (b * QC + cc) * NQ + m + 1)
                            for s in range(PARTS):
                                if m < KC:
                                    dst = qparts[l][bass.ds(b * H + m * (P // DH), P // DH), s * DH:(s + 1) * DH, bass.ts(cc, CH)]
                                    src = part[m][:, s, :]
                                elif l == 0:
                                    dst = kparts[l][bass.ds(b, 1), s * DH:(s + 1) * DH, bass.ts(cc, CH)]
                                    src = part[m][0:DH, s, :]
                                else:
                                    dst = kparts[l][bass.ds(b * NG, NG), s * DH:(s + 1) * DH, bass.ts(cc, CH)]
                                    src = part[m][:, s, :]
                                sp.dma_start(dst, src).then_inc(S["q_out"][m], 16)
                for m in range(NQ):
                    sp.wait_ge(S["q_out"][m], 16 * PARTS * NCH)

            def load_slot(l, it, u):
                S = L[l]
                n = it * SLOTS + u
                q = qparts[l][bass.ds(n * HG, HG), :, :] if not isinstance(n, int) else qparts[l][n * HG:(n + 1) * HG, :, :]
                kn = n if l else it // (ITERS // B)
                k = kparts[l][bass.ds(kn, 1), :, :]
                for row, rows in ((0, 3 * DH), (3 * DH, 2 * DH), (5 * DH, DH)):
                    for c in range(QC):
                        sp.dma_start(q_slot[u][row:row + rows, c, :, :],
                                     q[:, 0:rows, c * CH:(c + 1) * CH].rearrange("h r q -> r h q")).then_inc(S["slot_in"][u], 16)
                for row, s in ((0, 0), (1, 0), (2, 0), (3, 1), (4, 1), (5, 2)):
                    sp.dma_start(k_slot[u][row * DH:(row + 1) * DH, :],
                                 k[:, s * DH:(s + 1) * DH, :].rearrange("o d q -> (o d) q")).then_inc(S["slot_in"][u], 16)

            def max_rows(l, u, c, m):
                S = L[l]
                sp.wait_ge(S["m_ready"], m + 1)
                for s in range(MROWS):
                    sp.dma_start(q_slot[u][ROWS + s:ROWS + s + 1, c, :, :].rearrange("o h (t q) -> o (h t) q", q=P),
                                 negm[c][0:NX, s, :]).then_inc(S["m_in"][c], 16)

            def store_o(l, it, u, c):
                S = L[l]
                n = it * SLOTS + u
                sp.wait_ge(S["o_copied"], n * QC + c + 2)
                for h in range(HG):
                    sp.dma_start(numer[l][bass.ds(n * HG + h, 1), :, c * CH:(c + 1) * CH].rearrange("o d q -> (o d) q"),
                                 o_sb[c][32 * h:32 * h + DH, :]).then_inc(S["o_out"][c], 16)
                sp.dma_start(denom[l][bass.ds(n * HG, HG), c * CH:(c + 1) * CH],
                             o_sb[c][DH:P:32, :]).then_inc(S["o_out"][c], 16)

            def attention(l):
                S = L[l]
                for u in range(SLOTS - 1):
                    load_slot(l, 0, u)
                for c in range(QC):
                    max_rows(l, 0, c, c)

                def step(it, u, last):
                    n = it * SLOTS + u
                    final = last and u == SLOTS - 1
                    if not (last and u > 0):
                        v = (u + SLOTS - 1) % SLOTS
                        sp.wait_ge(S["pv_done"], n * per_group[l] + P_RING)
                        load_slot(l, it if u == 0 else it + 1, v)
                    for c in range(QC):
                        if not final:
                            max_rows(l, (u + 1) % SLOTS, c, (n + 1) * QC + c)
                        store_o(l, it, u, c)

                with sp.Fori(0, ITERS - 1) as it:
                    for u in range(SLOTS):
                        step(it, u, False)
                for u in range(SLOTS):
                    if u == 0:
                        load_output(l, 0)
                    if u == 2:
                        load_inverses(l, 0)
                    step(ITERS - 1, u, True)
                load_output(l, 1)
                load_inverses(l, 1)

            def load_output(l, b):
                S = L[l]
                for c in range(QC):
                    sp.wait_ge(S["o_out"][c], 80 * NG * (b + 1) + 16)
                heads = slice(b * H, (b + 1) * H)
                sp.dma_start(inv[b], denom[l][heads, :].rearrange("h (a n) -> (h a) n", n=H * N // P)).then_inc(S["den_in"][b], 16)
                for t in range(KC):
                    h0 = b * H + t * (P // DH)
                    sp.dma_start(xnT[:, t, b * N:(b + 1) * N],
                                 numer[l][h0:h0 + P // DH, :, :].rearrange("h d q -> (h d) q")).then_inc(S["num_in"][b * KC + t], 16)

            def load_inverses(l, b):
                S = L[l]
                heads = slice(b * H, (b + 1) * H)
                sp.wait_ge(S["inv_ready"], b + 1)
                sp.dma_start(inverse[l][heads, :].rearrange("h (a n) -> (h a) n", n=H * N // P), inv[b]).then_inc(S["inv_out"][b], 16)
                sp.wait_ge(S["inv_out"][b], 16)
                for t in range(KC):
                    for h in range(P // DH):
                        sp.dma_start(den[b][t][h * DH:(h + 1) * DH, :],
                                     inverse[l][b * H + t * (P // DH) + h, :].partition_broadcast(DH)).then_inc(S["num_in"][b * KC + t], 16)

            load_ffn0(range(0, 2))
            load_projections(0)
            load_ffn0(range(2, FT))
            for l in (0, 1):
                S = L[l]
                if l == 1:
                    sp.wait_ge(L[0]["y2_ready"], TT)
                    sp.wait_ge(L[0]["y2_evac"], TT)
                    load_projections(1)
                    load_ffn1()
                if l == 1:
                    sp.wait_ge(S["b_ready"], TT)
                    sp.dma_start(rope_cos, rcos).then_inc(rope_in, 16)
                    sp.dma_start(rope_sin, rsin).then_inc(rope_in, 16)
                store_parts(l)
                attention(l)
            S = L[1]
            for t in range(TT):
                sp.wait_ge(S["y2_evac"], t + 1)
                sp.dma_start(out[t * P:(t + 1) * P, :], res[t % 4]).then_inc(S["stored"][t % 4], 16)
            for s in S["stored"]:
                sp.wait_ge(s, 16 * TT // 4)

        @block.gpsimd
        def _(pool):
            pool.memset(ident[:, :], 0.0).then_inc(const_a, 1)
            pool.memset(identb[:, :], 0.0).then_inc(const_a, 1)
            pool.memset(mask_kq[:, :], 0.0).then_inc(const_a, 1)
            pool.memset(mask_qk[:, :], 0.0).then_inc(const_a, 1)
            pool.memset(v_all[:, :, :, DH:DH + 1], 1.0).then_inc(const_a, 1)
            pool.wait_ge(const_a, 5)
            for m in (ident, identb):
                pool.affine_select(out=m[:, :], in_=m[:, :], compare_op=ALU.not_equal, fill=1.0, base=0,
                                   pattern=[[-1, P]], channel_multiplier=1).then_inc(const_b, 1)
            pool.affine_select(out=mask_kq[:, :], in_=mask_kq[:, :], compare_op=ALU.is_ge, fill=MASKED, base=0,
                               pattern=[[1, P]], channel_multiplier=-1).then_inc(const_b, 1)
            pool.affine_select(out=mask_qk[:, :], in_=mask_qk[:, :], compare_op=ALU.is_ge, fill=MASKED, base=0,
                               pattern=[[-1, P]], channel_multiplier=1).then_inc(const_b, 1)
            for l in (0, 1):
                S = L[l]
                pool.wait_ge(S["wp_in"], 16 * (8 if l == 0 else 5))
                for t in range(TT):
                    pool.wait_ge(S["xn_ready"], t + 1)
                    pool.tensor_tensor(acc[:, t, :], acc[:, t, :], bias_o[:, :], ALU.add).then_inc(S["acc_biased"], 1)
                if l == 1:
                    pool.iota(topi[:, 0, :], pattern=[[1, E]], base=0, channel_multiplier=0).then_inc(iota_done, 1)
                    pool.wait_ge(iota_done, 1)
                    pool.tensor_copy(iota8, topi[:, 0, :]).then_inc(iota_done, 1)
                for c in range(NCH):
                    for m in range(NQ):
                        rows = DH if (m == KC and l == 0) else P
                        pool.wait_ge(S["rest_ready"], c * NQ + m + 1)
                        pool.tensor_copy(part[m][0:rows, 1, :], rest[m][0:rows, :]).then_inc(S["mid_done"], 1)
                        pool.wait_ge(S["mid_done"], c * NQ + m + 1)
                        pool.tensor_tensor(part[m][0:rows, 2, :], rest[m][0:rows, :], part[m][0:rows, 1, :],
                                           ALU.subtract).then_inc(S["lo_done"], 1)
                pool.wait_ge(S["v_done"], TT)
                pool.wait_ge(S["lo_done"], NCH * NQ)
                for m in range(NQ):
                    pool.wait_ge(S["q_out"][m], 16 * PARTS * NCH)

                def v_stage(it, u):
                    n = it * SLOTS + u
                    vn = n if l else it // (ITERS // B)
                    pool.tensor_copy(v_slot[u], v_all[:, vn, :, :]).then_inc(S["v_slot_ready"], 1)

                for u in range(SLOTS):
                    pool.memset(k_slot[u][ROWS:ROWS + MROWS, :], 1.0).then_inc(S["v_slot_ready"], 1)
                pool.wait_ge(S["v_slot_ready"], SLOTS)
                for u in range(SLOTS):
                    v_stage(0, u)
                for it in range(1, ITERS):
                    for u in range(SLOTS):
                        pool.wait_ge(S["pv_done"], (it * SLOTS + u - SLOTS + 1) * per_group[l] + P_RING)
                        v_stage(it, u)
                for t in range(KC):
                    pool.wait_ge(S["num_in"][t], 16 * (1 + P // DH))
                    o = xnT[:, t, 0:N]
                    pool.tensor_tensor(o, o, den[0][t], ALU.mult).then_inc(S["on_ready0"], 1)

        @block.scalar
        def _(act):
            for l in (0, 1):
                S = L[l]
                def deviation(g):
                    act.wait_ge(S["eps_done"], g + 1)
                    act.activation(std[:, g * TPC:(g + 1) * TPC], var[:, g * TPC:(g + 1) * TPC], ACT.Sqrt).then_inc(S["sqrt_done"], 1)

                def copy_T(g):
                    for t in range(g * TPC, (g + 1) * TPC):
                        act.wait_ge(S["xn_T"], t + 1)
                        act.activation(xnT[:, :, t * P:(t + 1) * P], bank(t % 2).rearrange("p (k q) -> p k q", k=KC), ACT.Copy).then_inc(S["xnT_ready"], 1)

                if l == 1:
                    deviation(0)
                    deviation(1)
                    deviation(2)
                    copy_T(0)
                    deviation(3)
                    copy_T(1)
                    copy_T(2)
                    copy_T(3)
                else:
                    for g in range(NCH):
                        deviation(g)
                        copy_T(g)
                if l == 0:
                    def x_high(p, tokens):
                        act.activation(x_hi[:, p, :, :], xnT[:, :, tokens], ACT.Copy).then_inc(S["xhi_done"], 1)

                    x_high(0, slice(0, CH))
                    for r, js in enumerate(ROUNDS):
                        for n, j in enumerate(js):
                            act.wait_ge(S["raw_in"][j % 2], 48 * (j // 2 + 1))
                            if r:
                                act.wait_ge(S["y_ready"], TT * r)
                            for raw, hi in zip(weight_views(w_raw[:, j % 2, :], j), weight_views(w_hi[:, n, :], j)):
                                act.activation(hi, raw, ACT.Copy).then_inc(S["whi_done"], 1)
                        with act.Fori(0, NCH // 2) as i:
                            for half in range(2):
                                base = NCH * W_SLOTS * r + (2 * i + half) * len(js)
                                for n, j in enumerate(js):
                                    w = width_f(j)
                                    act.wait_ge(S["gu_ready"], base + n + 1)
                                    act.activation(sil[0:w, n % 2, :], bank(n % 2)[0:w, :], ACT.Silu).then_inc(S["silu_done"], 1)
                                    if n == 0:
                                        x_high(1 - half, bass.ds(i * CH * 2 + CH, CH) if half == 0 else bass.ds(i * (-CH * 2) + CH * 2, CH))
                else:
                    for t in range(TT):
                        act.wait_ge(S["hl_ready"], t + 1)
                        act.activation(hl[:, t, :], bank(t % 2)[:, 0:E * R + E], ACT.Copy).then_inc(S["hl_sb"], 1)
                    act.wait_ge(S["gap_done"], 1)
                    act.activation(egap, gap, ACT.Exp).then_inc(S["egap_done"], 1)
                    for t in range(TT):
                        act.wait_ge(S["hwT_ready"], t + 1)
                        act.activation(hwT[:, t, :], bank(2 + t % 2)[:, 0:P], ACT.Copy).then_inc(S["hwT_sb"], 1)
                if l == 0:
                    act.wait_ge(S["wp_in"], 16 * 8)
                for c in range(NCH):
                    if c:
                        act.wait_ge(S["rest_ready"], c * NQ)
                    for m in range(NQ):
                        rows = DH if (m == KC and l == 0) else P
                        bias = 0.0 if l else (bias_q[:, m:m + 1] if m < KC else bias_k[:, 0:1])
                        act.wait_ge(S["q_ready"], c * NQ + m + 1)
                        act.activation(q32[m][0:rows, :], bank(m)[0:rows, :], ACT.Identity, bias=bias).then_inc(S["q32_ready"], 1)

                items = [main_items(l == 1, c) for c in range(QC)]
                group_items = per_group[l]
                for m in range(NQ):
                    act.wait_ge(S["q_out"][m], 16 * PARTS * NCH)
                for c in range(QC):
                    act.sem_inc(S["o_out"][c], 16)
                act.sem_inc(S["p_ready"], SP_RING)

                def attend(it):
                    base = it * (SLOTS * group_items)
                    local = 0

                    def copy_o(u, c, through):
                        n = it * SLOTS + u
                        act.wait_ge(S["pv_done"], base + through + P_RING)
                        act.wait_ge(S["o_out"][c], n * 80 + 16)
                        act.activation(o_sb[c], bank(7), ACT.Copy).then_inc(S["o_copied"], 1)

                    before = None
                    for u in range(SLOTS):
                        for c in range(QC):
                            for i, (kt, h, q0) in enumerate(items[c]):
                                act.wait_ge(S["s_ready"], base + local + 1)
                                act.wait_ge(S["pv_done"], base + local + 1)
                                act.activation(prob[local % P_RING][:, q0:CH], bank(local % SP_RING)[:, q0:CH],
                                               ACT.Exp, scale=SCALE).then_inc(S["p_ready"], 1)
                                local += 1
                                if i == 1 and before:
                                    copy_o(*before)
                            before = (u, c, local)
                    copy_o(*before)

                with act.Fori(0, ITERS - 1) as it:
                    attend(it)
                attend(ITERS - 1)

        @block.vector
        def _(dve):
            made = [0]

            def chained(ins):
                ins.then_inc(dve_chain, 1)
                made[0] += 1

            def wait_chain():
                dve.wait_ge(dve_chain, made[0])

            def normalise(l, g):
                S = L[l]
                ts = range(g * TPC, (g + 1) * TPC)
                q = slice(g * TPC, (g + 1) * TPC)
                for t in ts:
                    chained(dve.bn_stats(stats[:, t, :], acc[:, t, :]))
                wait_chain()
                for t in ts:
                    chained(dve.bn_aggr(mv[:, t, :], stats[:, t, :]))
                wait_chain()
                dve.tensor_scalar(var[:, q], mv[:, q, 1], EPS, None, ALU.add).then_inc(S["eps_done"], 1)
                dve.wait_ge(S["sqrt_done"], g + 1)
                chained(dve.reciprocal(rstd[:, q], std[:, q]))
                wait_chain()
                chained(dve.tensor_tensor(nwt[:, q], rstd[:, q], rstd[:, q], ALU.mult))
                wait_chain()
                chained(dve.tensor_tensor(std[:, q], nwt[:, q], var[:, q], ALU.mult))
                wait_chain()
                chained(dve.tensor_scalar(nwt[:, q], std[:, q], -0.5, 1.5, ALU.mult, ALU.add))
                wait_chain()
                chained(dve.tensor_tensor(std[:, q], rstd[:, q], nwt[:, q], ALU.mult))
                wait_chain()
                for t in ts:
                    if t >= XN_RING:
                        dve.wait_ge(S["xn_T"], t - XN_RING + 1)
                    dve.tensor_scalar(xn[l][t % XN_RING], acc[:, t, :], mv[:, t, 0:1], std[:, t:t + 1], ALU.subtract,
                                      ALU.mult).then_inc(S["xn_ready"], 1)

            for g in range(NCH):
                dve.wait_ge(x_in[g], 16)
                normalise(0, g)
            for l in (0, 1):
                S = L[l]
                if l == 0:
                    def x_low(p, tokens, n):
                        dve.wait_ge(S["xhi_done"], n)
                        dve.tensor_tensor(x_lo[:, p, :, :], xnT[:, :, tokens], x_hi[:, p, :, :].bitcast(F32),
                                          ALU.subtract).then_inc(S["xc_ready"], 1)

                    dve.wait_ge(S["xnT_ready"], TT)
                    x_low(0, slice(0, CH), 1)
                    for r, js in enumerate(ROUNDS):
                        for n, j in enumerate(js):
                            dve.wait_ge(S["whi_done"], 2 * (j + 1))
                            last = None
                            for raw, hi, lo in zip(weight_views(w_raw[:, j % 2, :], j), weight_views(w_hi[:, n, :], j),
                                                   weight_views(w_lo[:, n, :], j)):
                                last = dve.tensor_tensor(lo, raw, hi.bitcast(F32), ALU.subtract)
                            last.then_inc(S["w_ready"], 1)
                        with dve.Fori(0, NCH // 2) as i:
                            for half in range(2):
                                chunk = 2 * i + half
                                base = NCH * W_SLOTS * r + chunk * len(js)
                                for n, j in enumerate(js):
                                    w = width_f(j)
                                    dve.wait_ge(S["silu_done"], base + n + 1)
                                    dve.tensor_tensor(hid[0:w, n % 2, :], sil[0:w, n % 2, :], bank(2 + n % 2)[0:w, :], ALU.mult).then_inc(S["prod_done"], 1)
                                    dve.wait_ge(S["prod_done"], base + n + 1)
                                    dve.tensor_copy(h_hi[0:w, n % 2, :], hid[0:w, n % 2, :]).then_inc(S["hhi_done"], 1)
                                    dve.wait_ge(S["hhi_done"], base + n + 1)
                                    dve.tensor_tensor(h_lo[0:w, n % 2, :], hid[0:w, n % 2, :], h_hi[0:w, n % 2, :].bitcast(F32),
                                                      ALU.subtract).then_inc(S["hid_done"], 1)
                                    if n == 0:
                                        x_low(1 - half, bass.ds(i * CH * 2 + CH, CH) if half == 0 else bass.ds(i * (-CH * 2) + CH * 2, CH),
                                              NCH * r + chunk + 2)
                                for t in range(TPC):
                                    tile = chunk * TPC + t
                                    dve.wait_ge(S["acc_biased"], tile + 1)
                                    dve.wait_ge(S["y_ready"], TT * r + tile + 1)
                                    a = acc[:, bass.ds(tile, 1), :].rearrange("p o d -> p (o d)")
                                    dve.tensor_tensor(a, a, bank(4 + t), ALU.add).then_inc(S["y_evac"], 1)
                else:
                    dve.wait_ge(iota_done, 2)
                    dve.wait_ge(S["hl_sb"], TT)
                    lg = hl[:, :, E * R:E * R + E]
                    for t in range(TT):
                        dve.max(top[:, t, :], lg[:, t, :]).then_inc(dve_chain, 1)
                        made[0] += 1
                    dve.wait_ge(dve_chain, made[0])
                    dve.tensor_tensor(gap, top[:, :, 1], top[:, :, 0], ALU.subtract).then_inc(S["gap_done"], 1)
                    for t in range(TT):
                        dve.max_index(topi[:, t, :], top[:, t, :], lg[:, t, :]).then_inc(dve_chain, 1)
                        made[0] += 1
                    dve.wait_ge(dve_chain, made[0])
                    dve.tensor_copy(topf, topi[:, :, 0:2]).then_inc(dve_chain, 1)
                    made[0] += 1
                    dve.wait_ge(S["egap_done"], 1)
                    dve.tensor_scalar(esum, egap, 1.0, None, ALU.add).then_inc(dve_chain, 1)
                    made[0] += 1
                    dve.wait_ge(dve_chain, made[0])
                    dve.reciprocal(winv, esum).then_inc(dve_chain, 1)
                    made[0] += 1
                    dve.wait_ge(dve_chain, made[0])
                    dve.tensor_scalar(wt1, winv, 2.0, None, ALU.mult).then_inc(dve_chain, 1)
                    made[0] += 1
                    dve.wait_ge(dve_chain, made[0])
                    dve.tensor_tensor(wt2, wt1, egap, ALU.mult).then_inc(dve_chain, 1)
                    made[0] += 1
                    dve.wait_ge(dve_chain, made[0])
                    dve.wait_ge(dve_chain, made[0])
                    for t in range(TT):
                        dve.tensor_scalar(gate1[:, t, :], iota8, topf[:, t, 0:1], wt1[:, t:t + 1], ALU.is_equal, ALU.mult).then_inc(dve_chain, 1)
                        made[0] += 1
                        dve.tensor_scalar(gate2[:, t, :], iota8, topf[:, t, 1:2], wt2[:, t:t + 1], ALU.is_equal, ALU.mult).then_inc(dve_chain, 1)
                        made[0] += 1
                    dve.wait_ge(dve_chain, made[0])
                    dve.tensor_tensor(gate, gate1, gate2, ALU.add).then_inc(dve_chain, 1)
                    made[0] += 1
                    dve.wait_ge(dve_chain, made[0])
                    for t in range(TT):
                        g = gate[:, t, :].rearrange("p (e o) -> p e o", o=1).to_broadcast([P, E, R])
                        dve.tensor_tensor(hw[:, t, :].rearrange("p (e r) -> p e r", e=E),
                                          hl[:, t, 0:E * R].rearrange("p (e r) -> p e r", e=E), g, ALU.mult).then_inc(S["hw_done"], 1)
                    for t in range(TT):
                        dve.wait_ge(S["acc_biased"], t + 1)
                        dve.wait_ge(S["b_ready"], t + 1)
                        dve.tensor_tensor(acc[:, t, :], acc[:, t, :], bank(4 + t % 4), ALU.add).then_inc(S["b_evac"], 1)

                if l:
                    dve.wait_ge(rope_in, 32)
                for c in range(NCH):
                    pos = slice(c % QC * CH, (c % QC + 1) * CH)
                    for m in range(NQ):
                        rows = DH if (m == KC and l == 0) else P
                        dve.wait_ge(S["q32_ready"], c * NQ + m + 1)
                        if c:
                            dve.wait_ge(S["q_out"][m], c * (16 * PARTS))
                        if l:
                            dve.stream_shuffle(rest[m], q32[m], swap).then_inc(dve_chain, 1)
                            made[0] += 1
                            dve.wait_ge(dve_chain, made[0])
                            dve.tensor_tensor(q32[m], q32[m], rope_cos[:, pos], ALU.mult).then_inc(dve_chain, 1)
                            dve.tensor_tensor(rest[m], rest[m], rope_sin[:, pos], ALU.mult).then_inc(dve_chain, 1)
                            made[0] += 2
                            dve.wait_ge(dve_chain, made[0])
                            dve.tensor_tensor(q32[m], q32[m], rest[m], ALU.add).then_inc(dve_chain, 1)
                            made[0] += 1
                            dve.wait_ge(dve_chain, made[0])
                        dve.tensor_copy(part[m][0:rows, 0, :], q32[m][0:rows, :]).then_inc(S["hi_done"], 1)
                        dve.wait_ge(S["hi_done"], c * NQ + m + 1)
                        dve.tensor_tensor(rest[m][0:rows, :], q32[m][0:rows, :], part[m][0:rows, 0, :], ALU.subtract).then_inc(S["rest_ready"], 1)
                for t in range(TT):
                    b, kt = divmod(t, KT)
                    kv = (1, NG)[l]
                    dve.wait_ge(S["v_ready"], t + 1)
                    dst = v_all[:, b * kv:(b + 1) * kv, kt, 0:DH]
                    src = bank(5 + t % 3)[:, 0:KVW[l]].rearrange("p (h d) -> p h d", h=kv)
                    if l == 0:
                        dve.tensor_tensor(dst, src, bias_v[:, :].rearrange("p (h d) -> p h d", h=1), ALU.add).then_inc(S["v_done"], 1)
                    else:
                        dve.tensor_copy(dst, src).then_inc(S["v_done"], 1)

                for m in range(NQ):
                    dve.wait_ge(S["q_out"][m], 16 * PARTS * NCH)

                def maxima(n):
                    for e, (c, qt, h) in enumerate(max_items()):
                        j = n * (QC * XI) + e
                        src = bank(3 + 2 * (e % 2), 2)
                        dve.wait_ge(S["x_ready"], j + 1)
                        if qt is not None:
                            dve.tensor_reduce(maxes[c][:, h * TPC + qt:h * TPC + qt + 1], src[:, 0:max_width(l == 1, c, qt)],
                                              AX_X, ALU.max).then_inc(S["x_done"], 1)
                            continue
                        if not (isinstance(n, int) and n == 0):
                            dve.wait_ge(S["m_in"][c], n * (16 * MROWS))
                        mt = src[0:NX, 0:P]
                        dve.tensor_scalar(negm[c][0:NX, 0, :], mt, -1.0, None, ALU.mult).then_inc(S["mhi_done"], 1)
                        dve.wait_ge(S["mhi_done"], n * QC + c + 1)
                        dve.scalar_tensor_tensor(negm[c][0:NX, 1, :], mt, -1.0, negm[c][0:NX, 0, :], ALU.mult,
                                                 ALU.subtract).then_inc(S["m_ready"], 1)
                        dve.wait_ge(S["m_ready"], n * QC + c + 1)
                        dve.sem_inc(S["x_done"], 1)

                maxima(0)
                def invert(b):
                    dve.wait_ge(S["den_in"][b], 16)
                    dve.reciprocal(inv[b], inv[b]).then_inc(S["inv_ready"], 1)

                with dve.Fori(1, B * NG - 1) as n:
                    maxima(n)
                invert(0)
                maxima(B * NG - 1)

                invert(1)
                for t in range(KC):
                    dve.wait_ge(S["num_in"][KC + t], 16 * (1 + P // DH))
                    o = xnT[:, t, N:2 * N]
                    dve.tensor_tensor(o, o, den[1][t], ALU.mult).then_inc(S["on_ready1"], 1)
                for t in range(TT):
                    dve.wait_ge(S["y2_ready"], t + 1)
                    if l == 0:
                        dve.tensor_tensor(acc[:, t, :], acc[:, t, :], bank(t % 8), ALU.add).then_inc(S["y2_evac"], 1)
                        if t % TPC == TPC - 1:
                            dve.wait_ge(S["y2_evac"], t + 1)
                            normalise(1, t // TPC)
                    else:
                        if t >= 4:
                            dve.wait_ge(S["stored"][t % 4], 16 * (t // 4))
                        dve.tensor_tensor(res[t % 4], acc[:, t, :], bank(t % 8), ALU.add).then_inc(S["y2_evac"], 1)

        @block.tensor
        def _(pe):
            pe.wait_ge(const_b, 4)
            for l in (0, 1):
                S = L[l]
                if l == 1:
                    pe.wait_ge(L[0]["y2_evac"], 10)
                for t in range(TT):
                    pe.wait_ge(S["xn_ready"], t + 1)
                    if t >= 2:
                        pe.wait_ge(S["xnT_ready"], t - 1)
                    for k in range(KC):
                        last = pe.transpose(bank(t % 2)[:, k * P:(k + 1) * P], xn[l][t % XN_RING][:, k * P:(k + 1) * P], ident[:, :])
                    last.then_inc(S["xn_T"], 1)
                pe.wait_ge(S["xnT_ready"], TT)
                if l == 1:
                    pe.wait_ge(L[0]["y2_evac"], TT)
                if l == 0:
                    pe.sem_inc(S["hid_done"], 1)
                    pe.sem_inc(S["y_evac"], 1)

                    def chunk_of_round(r, js, c, p):
                        base = NCH * W_SLOTS * r + c * len(js)

                        def passes(out_, hi_w, lo_w, hi_x, lo_x, start, stop):
                            pe.matmul(out_, hi_w, hi_x, start=start, stop=False)
                            pe.matmul(out_, hi_w, lo_x, start=False, stop=False)
                            return pe.matmul(out_, lo_w, hi_x, start=False, stop=stop)

                        def down(n):
                            w = width_f(js[n])
                            pe.wait_ge(S["hid_done"], base + n + 2)
                            if n == 0:
                                pe.wait_ge(S["y_evac"], TT * r + c * TPC + 1)
                            for t in range(TPC):
                                q = slice(t * P, (t + 1) * P)
                                last = passes(bank(4 + t), h_hi[0:w, n % 2, q], h_lo[0:w, n % 2, q], w_hi[0:w, n, GU:GU + D],
                                              w_lo[0:w, n, GU:GU + D], n == 0, n == len(js) - 1)
                                if n == len(js) - 1:
                                    last.then_inc(S["y_ready"], 1)

                        pe.wait_ge(S["xc_ready"], NCH * r + c + 1)
                        for n, j in enumerate(js):
                            w = width_f(j)
                            pe.wait_ge(S["w_ready"], j + 1)
                            pe.wait_ge(S["hid_done"], base + max(1, n))
                            for g in range(2):
                                for k in range(KC):
                                    f0 = (2 * k + g) * P
                                    last = passes(bank(2 * g + n % 2)[0:w, :], w_hi[:, n, f0:f0 + w], w_lo[:, n, f0:f0 + w],
                                                  x_hi[:, p, k, :], x_lo[:, p, k, :], k == 0, k == KC - 1)
                            last.then_inc(S["gu_ready"], 1)
                            if n >= 1:
                                down(n - 1)
                        down(len(js) - 1)

                    for r, js in enumerate(ROUNDS):
                        with pe.Fori(0, NCH // 2) as i:
                            for half in range(2):
                                chunk_of_round(r, js, 2 * i + half, half)
                else:
                    pe.wait_ge(S["wf_in"], 16 * 4)
                    for t in range(TT):
                        if t >= 2:
                            pe.wait_ge(S["hl_sb"], t - 1)
                        for k in range(KC):
                            last = pe.matmul(bank(t % 2)[:, 0:E * R + E], xnT[:, k, t * P:(t + 1) * P], w_ar[:, k, :],
                                             start=(k == 0), stop=(k == KC - 1))
                        last.then_inc(S["hl_ready"], 1)
                    for t in range(TT):
                        pe.wait_ge(S["hw_done"], t + 1)
                        if t >= 2:
                            pe.wait_ge(S["hwT_sb"], t - 1)
                        pe.transpose(bank(2 + t % 2)[:, 0:P], hw[:, t, :], ident[:, :]).then_inc(S["hwT_ready"], 1)
                    for t in range(TT):
                        if t >= 4:
                            pe.wait_ge(S["b_evac"], t - 3)
                        for k in range(KC):
                            pe.matmul(bank(4 + t % 4), xnT[:, k, t * P:(t + 1) * P], w_base[:, k, :], start=(k == 0), stop=False)
                        pe.wait_ge(S["hwT_sb"], t + 1)
                        pe.matmul(bank(4 + t % 4), hwT[:, t, :], w_lb, start=False, stop=True).then_inc(S["b_ready"], 1)

                pe.wait_ge(S["wp_in"], 16 * (8 if l == 0 else 5))
                if l == 0:
                    pe.wait_ge(S["y_evac"], TT * len(ROUNDS) + 1)
                else:
                    pe.wait_ge(S["b_evac"], TT)
                kw = KVW[l]
                for c in range(NCH):
                    if c:
                        pe.wait_ge(S["q32_ready"], c * NQ)
                    for m in range(NQ):
                        for k in range(KC):
                            w = w_q[:, k, m * P:(m + 1) * P] if m < KC else w_kv[:, k, 0:kw]
                            last = pe.matmul(bank(m) if m < KC else bank(m)[0:kw, :], w, xnT[:, k, c * CH:(c + 1) * CH],
                                             start=(k == 0), stop=(k == KC - 1))
                        last.then_inc(S["q_ready"], 1)
                for t in range(TT):
                    if t >= 3:
                        pe.wait_ge(S["v_done"], t - 2)
                    for k in range(KC):
                        last = pe.matmul(bank(5 + t % 3)[:, 0:kw], xnT[:, k, t * P:(t + 1) * P], w_kv[:, k, kw:2 * kw],
                                         start=(k == 0), stop=(k == KC - 1))
                    last.then_inc(S["v_ready"], 1)
                pe.wait_ge(S["v_done"], TT)
                pe.wait_ge(S["q32_ready"], NCH * NQ)

                causal = l == 1
                items = [main_items(causal, c) for c in range(QC)]
                group_items = per_group[l]
                pe.sem_inc(S["o_copied"], 1)
                pe.sem_inc(S["pv_done"], P_RING)

                XL = max_items()

                def max_pieces():
                    r = []
                    for e, (c, qt, h) in enumerate(XL):
                        w = 1 if qt is None else max_width(causal, c, qt)
                        r += [(e, k0, min(w, k0 + CH), w) for k0 in range(0, w, CH)]
                    return r

                XP = max_pieces()

                def max_piece(n, u, piece):
                    e, k0, k1, w = piece
                    c, qt, h = XL[e]
                    dst = bank(3 + 2 * (e % 2), 2)
                    j = n * len(XL) + e
                    if k0 == 0 and not (isinstance(j, int) and j < 2):
                        pe.wait_ge(S["x_done"], j - 1 if e < len(XL) - 1 else j)
                    if qt is None:
                        pe.transpose(dst[0:NX, 0:P], maxes[c], ident[:, :]).then_inc(S["x_ready"], 1)
                        return
                    diag = causal and k1 == w
                    last = pe.matmul(dst[:, k0:k1], q_slot[u][0:ROWS, c, h, qt * P:(qt + 1) * P], k_slot[u][0:ROWS, k0:k1],
                                     start=True, stop=not diag)
                    if diag:
                        last = pe.matmul(dst[:, w - P:w], identb[:, :], mask_qk[:, :], start=False, stop=True)
                    if k1 == w:
                        last.then_inc(S["x_ready"], 1)

                def attend(it, last_iter):
                    base = it * (SLOTS * group_items)
                    pending = []
                    local = 0

                    def pv():
                        idx, u, c, kt, h, q0, nkt = pending.pop(0)
                        pe.wait_ge(S["p_ready"], base + idx + 1 + SP_RING)
                        if kt == 0 and h == 0:
                            pe.wait_ge(S["o_copied"], (it * SLOTS + u) * QC + c + 1)
                        mm = pe.matmul(bank(7)[32 * h:32 * h + DH + 1, q0:CH], v_slot[u][:, kt, :], prob[idx % P_RING][:, q0:CH],
                                       start=(kt == 0), stop=(kt == nkt - 1), tile_position=(0, 32 * h))
                        mm.then_inc(S["pv_done"], 1)

                    for u in range(SLOTS):
                        n = it * SLOTS + u
                        has_next = not (last_iter and u == SLOTS - 1)
                        v = (u + 1) % SLOTS
                        if has_next:
                            itv = it if u + 1 < SLOTS else it + 1
                            pe.wait_ge(S["slot_in"][v], (itv + 1) * (16 * 12))
                        pe.wait_ge(S["v_slot_ready"], n + 1 + SLOTS)
                        done = 0
                        i_g = 0
                        for c in range(QC):
                            nkt = len(items[c]) // HG
                            for i, (kt, h, q0) in enumerate(items[c]):
                                if i == 0:
                                    pe.wait_ge(S["m_in"][c], (n + 1) * (16 * MROWS))
                                slot = local % SP_RING
                                free = local if local >= SP_RING else first_free[local]
                                pe.wait_ge(S["p_ready"], base + free + 1)
                                diag = causal and kt >= TPC * c
                                mm = pe.matmul(bank(slot)[:, q0:CH], k_slot[u][0:ROWS + MROWS, kt * P:(kt + 1) * P],
                                               q_slot[u][0:ROWS + MROWS, c, h, q0:CH], start=True, stop=not diag)
                                if diag:
                                    mm = pe.matmul(bank(slot)[:, q0:q0 + P], identb[:, :], mask_kq[:, :], start=False, stop=True)
                                mm.then_inc(S["s_ready"], 1)
                                pending.append((local, u, c, kt, h, q0, nkt))
                                local += 1
                                i_g += 1
                                if has_next:
                                    due = min(len(XP) - 1, int(i_g * len(XP) / (0.93 * group_items)))
                                    if i_g == group_items:
                                        due = len(XP)
                                    while done < due:
                                        max_piece(n + 1, v, XP[done])
                                        done += 1
                                if len(pending) > LAG:
                                    pv()
                    while pending:
                        pv()

                total = SLOTS * group_items
                first_free = []
                for s in range(SP_RING):
                    lastuse = max(i for i in range(total) if i % SP_RING == s) - total
                    first_free.append(lastuse + SP_RING)

                pe.wait_ge(S["slot_in"][0], 16 * 12)
                pe.wait_ge(S["v_slot_ready"], SLOTS)
                for piece in XP:
                    max_piece(0, 0, piece)
                with pe.Fori(0, ITERS - 1) as it:
                    attend(it, False)
                attend(ITERS - 1, True)

                pe.wait_ge(S["o_copied"], B * NG * QC + 1)
                for t in range(TT):
                    pe.wait_ge(S["on_ready0"] if t < KT else S["on_ready1"], KC)
                    if t >= 8:
                        pe.wait_ge(S["y2_evac"], t - 7)
                    for k in range(KC):
                        last = pe.matmul(bank(t % 8), xnT[:, k, t * P:(t + 1) * P], w_o[:, k, :], start=(k == 0), stop=(k == KC - 1))
                    last.then_inc(S["y2_ready"], 1)


def kernel(**inputs):
    import numpy as _np
    import concourse.bacc as _bacc
    from concourse import mybir as _mybir
    from concourse.bass_utils import run_bass_kernel_spmd as _run

    def flat(name):
        return _np.ascontiguousarray(inputs[name])

    lb = flat("L1_ffn_lora_B")
    laid = {
        "x": flat("L0_attn_x").reshape(T, D),
        "wq0": flat("L0_attn_Wq"), "bq0": _np.ascontiguousarray(flat("L0_attn_bq").reshape(KC, P).T), "wk0": flat("L0_attn_Wk"), "bk0": flat("L0_attn_bk"),
        "wv0": flat("L0_attn_Wv"), "bv0": flat("L0_attn_bv"), "wo0": flat("L0_attn_Wo"), "bo0": flat("L0_attn_bo"),
        "wgu": _np.ascontiguousarray(flat("L0_ffn_w_gate_up").T), "wdn": _np.ascontiguousarray(flat("L0_ffn_w_down").T),
        "wq1": flat("L1_attn_Wq"), "wk1": flat("L1_attn_Wk"), "wv1": flat("L1_attn_Wv"), "wo1": flat("L1_attn_Wo"),
        "wbase": _np.ascontiguousarray(flat("L1_ffn_W_base").T), "bbase": flat("L1_ffn_b_base"),
        "wrt": _np.ascontiguousarray(flat("L1_ffn_W_router").T),
        "la": _np.ascontiguousarray(flat("L1_ffn_lora_A").reshape(E * R, D).T),
        "lb": _np.ascontiguousarray(lb.transpose(0, 2, 1)).reshape(E * R, D),
    }
    freq = (_np.float32(1.0) / _np.float32(10000.0) ** (_np.arange(0, DH, 2, dtype=_np.float32) / _np.float32(DH))).astype(_np.float32)
    angle = (_np.arange(N, dtype=_np.float32)[None, :] * _np.tile(_np.repeat(freq, 2), P // DH)[:, None]).astype(_np.float32)
    sign = _np.where(_np.arange(P) % 2 == 0, -1.0, 1.0).astype(_np.float32)
    laid["rcos"] = _np.cos(angle).astype(_np.float32)
    laid["rsin"] = (_np.sin(angle) * sign[:, None]).astype(_np.float32)
    nc = _bacc.Bacc("TRN2", target_bir_lowering=False, num_devices=1)
    arrays, args = {}, []
    for name, a in laid.items():
        arrays[f"in_{name}"] = a
        args.append(nc.dram_tensor(f"in_{name}", a.shape, _mybir.dt.from_np(a.dtype), kind="ExternalInput").ap())
    args.append(nc.dram_tensor("out_0", (T, D), F32, kind="ExternalOutput").ap())
    build(nc, *args)
    r = _run(nc, [arrays], core_ids=[0])
    return r.results[0]["out_0"].reshape(B, N, D)
```

```python
from contextlib import ExitStack

import concourse.bass as bass
from concourse import mybir

ALU = mybir.AluOpType
ACT = mybir.ActivationFunctionType
BF16 = mybir.dt.bfloat16
F32 = mybir.dt.float32
F32R = mybir.dt.float32r
U32 = mybir.dt.uint32
AX_X = mybir.AxisListType.X

P = 128
B, N, D = 2, 1024, 512
T = B * N
TT = T // P
KC = D // P
CH = 512
NCH = T // CH
H, DH = 32, 16
HG = 4
NG = H // HG
KT = N // P
QC = N // CH
TPC = CH // P
F = 1376
FT = -(-F // P)
E, R = 8, 16
W_SLOTS = 3
ROUNDS = [list(range(j, min(j + W_SLOTS, FT))) for j in range(0, FT, W_SLOTS)]
EPS = 1e-5
SCALE = 1.0 / DH ** 0.5
MASKED = -1e30
SLOTS = 4
ITERS = B * NG // SLOTS
SP_RING, P_RING, LAG = 3, 8, 3
MID_LAG = 2
PARTS = 3
ROWS = 6 * DH
MROWS = 2
XN_RING = [8, TT]
NX = TPC * HG
XI = NX + 1
MAX_END = [0.98, 0.95]
TAIL = [11, 0]


def width_f(j):
    return min(P, F - j * P)


def main_items(causal, qc):
    kts = TPC * (qc + 1) if causal else KT
    return [(kt, h, max(0, kt - TPC * qc) * P if causal else 0) for kt in range(kts) for h in range(HG)]


def weight_views(t, j):
    w = width_f(j)
    gu = KC * 2 * P
    return (t[:, 0:gu].rearrange("p (q c) -> p q c", c=P)[:, :, 0:w], t[0:w, gu:gu + D])


def max_items():
    r = [[(c, qt, h) for qt in range(TPC) for h in range(HG)] for c in range(QC)]
    return r[0] + r[1][:2] + [(0, None, None)] + r[1][2:] + [(1, None, None)]


def max_width(causal, qc, qt):
    return (TPC * qc + qt + 1) * P if causal else N


def build(nc, x, wq0, bq0, wk0, bk0, wv0, bv0, wo0, bo0, wgu, wdn, wq1, wk1, wv1, wo1,
          wbase, bbase, wrt, la, lb, rcos, rsin, out):
    ctx = ExitStack()
    with ctx:
        def sb(name, shape, dt=F32):
            return ctx.enter_context(nc.sbuf_tensor(name, shape, dt))

        def sem(name):
            return ctx.enter_context(nc.semaphore(name))

        qparts = [nc.dram_tensor(f"qparts{l}", [B * H, PARTS * DH, N], BF16, kind="Internal").ap() for l in (0, 1)]
        kparts = [nc.dram_tensor(f"kparts{l}", [B * kv, PARTS * DH, N], BF16, kind="Internal").ap()
                  for l, kv in ((0, 1), (1, NG))]
        numer = [nc.dram_tensor(f"numer{l}", [B * H, DH, N], F32, kind="Internal").ap() for l in (0, 1)]
        inverse = [nc.dram_tensor(f"inverse{l}", [B * H, N], F32, kind="Internal").ap() for l in (0, 1)]
        denom = [nc.dram_tensor(f"denom{l}", [B * H, N], F32, kind="Internal").ap() for l in (0, 1)]

        acc = sb("acc", [P, TT, D])
        xnT = sb("xnT", [P, KC, T])
        w_q = sb("w_q", [P, KC, D])
        w_kv = sb("w_kv", [P, KC, 256])
        w_o = sb("w_o", [P, KC, D])
        bias_q = sb("bias_q", [P, KC])
        bias_kv = sb("bias_kv", [2 * DH, 1])
        bias_o = sb("bias_o", [P, D])
        v_all = sb("v_all", [P, B * NG, KT, DH + 1])
        ident = sb("ident", [P, P])
        identb = sb("identb", [P, P], BF16)
        mask_kq = sb("mask_kq", [P, P], BF16)
        mask_qk = sb("mask_qk", [P, P], BF16)
        iota8u = sb("iota8u", [P, E], U32)
        iota8 = sb("iota8", [P, E])
        stats = sb("stats", [P, TT, 6])
        mv = sb("mv", [P, TT, 2])
        var = sb("var", [P, TT])
        std = sb("std", [P, TT])
        rstd = sb("rstd", [P, TT])
        nwt = sb("nwt", [P, TT])
        with ExitStack() as own:
            def fb(name, shape, dt=F32):
                return own.enter_context(nc.sbuf_tensor(name, shape, dt))

            GU = KC * 2 * P
            w_hi = fb("w_hi", [P, W_SLOTS, GU + D], F32R)
            w_lo = fb("w_lo", [P, W_SLOTS, GU + D], F32R)
            h_hi = fb("h_hi", [P, 2, CH], F32R)
            h_lo = fb("h_lo", [P, 2, CH], F32R)
            w_raw = fb("w_raw", [P, 2, GU + D])
            x_hi = fb("x_hi", [P, 2, KC, CH], F32R)
            x_lo = fb("x_lo", [P, 2, KC, CH], F32R)
            wo_hi, wo_lo = x_hi[:, 0, :, :], x_hi[:, 1, :, :]
            xo_hi = w_hi[:, :, :].rearrange("p n f -> p (n f)")[:, 0:2 * KC * CH].rearrange("p (i k q) -> p i k q", i=2, k=KC)
            xo_lo = x_lo
            xn0 = fb("xn0", [P, XN_RING[0], D])
            sil = xn0[:, 0:2, :]
            hid = xn0[:, 2:4, :]
        AR = 25 * 1024
        arena = sb("arena", [P, AR])

        used = [0]

        def region(cols, dt=F32, parts=P):
            a = used[0]
            used[0] += cols
            assert used[0] <= AR, used[0]
            v = arena[0:parts, a:a + cols]
            return v if dt == F32 else v.bitcast(dt)

        used[0] = W_SLOTS * (GU + D)
        xn = [[xn0[:, i, :] for i in range(XN_RING[0])], [region(D) for _ in range(XN_RING[1])]]
        w_base = region(KC * D).rearrange("p (k f) -> p k f", k=KC)
        w_ar = region(KC * (E * R + E)).rearrange("p (k f) -> p k f", k=KC)
        w_lb = region(D)
        hl = region(TT * (E * R + E)).rearrange("p (t f) -> p t f", t=TT)
        hw = region(TT * E * R).rearrange("p (t f) -> p t f", t=TT)
        hwT = region(TT * P).rearrange("p (t f) -> p t f", t=TT)
        top = region(TT * 8).rearrange("p (t f) -> p t f", t=TT)
        topi = region(TT * 8, U32).rearrange("p (t f) -> p t f", t=TT)
        topf = region(TT * 2).rearrange("p (t f) -> p t f", t=TT)
        gap = region(TT)
        egap = region(TT)
        esum = region(TT)
        winv = region(TT)
        wt1 = region(TT)
        wt2 = region(TT)
        gate1 = region(TT * E).rearrange("p (t f) -> p t f", t=TT)
        gate2 = region(TT * E).rearrange("p (t f) -> p t f", t=TT)
        gate = region(TT * E).rearrange("p (t f) -> p t f", t=TT)
        NQ = KC + 1
        used[0] = 0
        q32 = [region(CH) for _ in range(NQ)]
        rest = [region(CH) for _ in range(NQ)]
        part = [region(PARTS * CH // 2, BF16).rearrange("p (s q) -> p s q", s=PARTS) for _ in range(NQ)]
        rope_cos = region(N)
        rope_sin = region(N)
        projection_end = used[0]
        used[0] = 0
        prob = [region(CH) for _ in range(P_RING)]
        o_sb = [region(CH) for _ in range(QC)]
        inv = [region(H * N // P) for _ in range(B)]
        den = [[], [region(N) for _ in range(KC)]]
        den[0].append(region(N))
        assert used[0] <= projection_end
        used[0] = projection_end
        den[0] += [region(N) for _ in range(KC - 1)]
        res = [den[0][i][:, 0:D] for i in range(4)]
        q_slot = [region(HG * N // 2, BF16).rearrange("p (c h q) -> p c h q", c=QC, h=HG) for _ in range(SLOTS)]
        k_slot = [region(N // 2, BF16) for _ in range(SLOTS)]
        v_slot = [region(KT * (DH + 1)).rearrange("p (k d) -> p k d", k=KT) for _ in range(SLOTS)]
        maxes = [region(NX) for _ in range(QC)]
        negm = [region(MROWS * P // 2, BF16).rearrange("p (s q) -> p s q", s=MROWS) for _ in range(QC)]

        ps = ctx.enter_context(nc.psum_tensor("ps", [P, 8 * CH], F32))

        def bank(i, n=1):
            return ps[:, i * CH:(i + n) * CH]

        def sems(l):
            names = (
                     "eps_done sqrt_done xn_ready xn_T xnT_ready acc_biased q_ready q32_ready hi_done rest_ready "
                     "mid_done lo_done v_ready v_done v_slot_ready s_ready p_ready pv_done o_copied x_ready "
                     "x_done mhi_done m_ready inv_ready on_ready0 on_ready1 y2_ready y2_evac wo_hi_done "
                     "wo_ready xo_hi_done xo_ready ").split()
            names += ((
                     "gu_ready silu_done prod_done hhi_done hid_done whi_done w_ready xhi_done xc_ready y_ready "
                     "y_evac ").split(), (
                     "hl_ready hl_sb gap_done egap_done hw_done hwT_ready hwT_sb b_ready b_evac ").split())[l]
            S = {n: sem(f"{n}_{l}") for n in names}
            S["q_out"] = [sem(f"q_out{m}_{l}") for m in range(NQ)]
            S["slot_in"] = [sem(f"slot_in{u}_{l}") for u in range(SLOTS)]
            S["m_in"] = [sem(f"m_in{c}_{l}") for c in range(QC)]
            S["o_out"] = [sem(f"o_out{c}_{l}") for c in range(QC)]
            S["den_in"] = [sem(f"den_in{b}_{l}") for b in range(B)]
            S["inv_out"] = [sem(f"inv_out{b}_{l}") for b in range(B)]
            S["num_in"] = [sem(f"num_in{i}_{l}") for i in range(B * KC)]
            S["raw_in"] = [sem(f"raw_in{i}_{l}") for i in range(2 - 2 * l)]
            S["stored"] = [sem(f"stored{i}_{l}") for i in range(4 * l)]
            S["wf_in"] = sem(f"wf_in_{l}")
            S["wp_in"] = sem(f"wp_in_{l}")
            return S

        L = [sems(0), sems(1)]
        x_in = [sem(f"x_in{g}") for g in range(NCH)]
        rope_in = sem("rope_in")
        bias_in = [sem("bias_in0"), sem("bias_in1")]
        swap = [i ^ 1 for i in range(32)]
        const_a = sem("const_a")
        const_b = sem("const_b")
        iota_done = sem("iota_done")
        dve_chain = sem("dve_chain")

        KVW = [DH, NG * DH]
        V_STEPS = [NCH, TT]
        per_group = [sum(len(main_items(l == 1, c)) for c in range(QC)) for l in (0, 1)]

        block = ctx.enter_context(nc.Block())

        @block.sync
        def _(sp):
            for g in range(NCH):
                sp.dma_start(acc[:, g * TPC:(g + 1) * TPC, :],
                             x[g * CH:(g + 1) * CH, :].rearrange("(t p) d -> p t d", p=P)).then_inc(x_in[g], 16)

            def load_projections(l):
                S = L[l]
                wq, wk, wv, wo = ((wq0, wk0, wv0, wo0), (wq1, wk1, wv1, wo1))[l]
                kw = KVW[l]
                r = "(k p) n -> p k n"
                sp.dma_start(w_q[:, :, :], wq.rearrange(r, p=P)).then_inc(S["wp_in"], 16)
                sp.dma_start(w_kv[:, :, 0:kw], wk.rearrange(r, p=P)).then_inc(S["wp_in"], 16)
                sp.dma_start(w_kv[:, :, kw:2 * kw], wv.rearrange(r, p=P)).then_inc(S["wp_in"], 16)
                sp.dma_start(w_o[:, :, :], wo.rearrange(r, p=P)).then_inc(S["wp_in"], 16)
                if l == 0:
                    sp.dma_start(bias_q[:, :], bq0).then_inc(S["wp_in"], 16)
                    sp.dma_start(bias_kv[0:DH, :], bk0.rearrange("(p a) -> p a", a=1)).then_inc(S["wp_in"], 16)
                    sp.dma_start(bias_kv[DH:2 * DH, :], bv0.rearrange("(p a) -> p a", a=1)).then_inc(S["wp_in"], 16)
                    sp.dma_start(bias_o[:, :], bo0.partition_broadcast(P)).then_inc(bias_in[0], 16)

            def load_ffn0(js):
                S = L[0]
                for j in js:
                    w = width_f(j)
                    raw = w_raw[:, j % 2, :]
                    gu = raw[:, 0:GU].rearrange("p (k g c) -> p k g c", k=KC, g=2)
                    if j >= 2:
                        sp.wait_ge(S["w_ready"], j - 1)
                    for g in range(2):
                        sp.dma_start(gu[:, :, g, 0:w], wgu[:, g * F + j * P:g * F + j * P + w].rearrange("(k p) n -> p k n", p=P)).then_inc(S["raw_in"][j % 2], 16)
                    sp.dma_start(raw[0:w, GU:GU + D], wdn[j * P:j * P + w, :]).then_inc(S["raw_in"][j % 2], 16)

            def load_ffn1():
                S = L[1]
                r = "(k p) n -> p k n"
                sp.dma_start(w_base, wbase.rearrange(r, p=P)).then_inc(S["wf_in"], 16)
                sp.dma_start(w_ar[:, :, 0:E * R], la.rearrange(r, p=P)).then_inc(S["wf_in"], 16)
                sp.dma_start(w_ar[:, :, E * R:E * R + E], wrt.rearrange(r, p=P)).then_inc(S["wf_in"], 16)
                sp.dma_start(w_lb, lb).then_inc(S["wf_in"], 16)

            def store_parts(l, b):
                S = L[l]
                with sp.Fori(0, QC) as cc:
                    for m in range(NQ):
                        sp.wait_ge(S["lo_done"], (b * QC + cc) * NQ + m + 1)
                        for s in range(PARTS):
                            rows = slice(s * DH, (s + 1) * DH)
                            if m < KC:
                                h0 = b * H + m * (P // DH)
                                dst, src = qparts[l][h0:h0 + P // DH, rows, bass.ts(cc, CH)], part[m][:, s, :]
                            elif l == 0:
                                dst, src = kparts[l][b:b + 1, rows, bass.ts(cc, CH)], part[m][0:DH, s, :]
                            else:
                                dst, src = kparts[l][b * NG:(b + 1) * NG, rows, bass.ts(cc, CH)], part[m][:, s, :]
                            sp.dma_start(dst, src).then_inc(S["q_out"][m], 16)

            def load_slot(l, it, u):
                S = L[l]
                n = it * SLOTS + u
                q = qparts[l][bass.ds(n * HG, HG), :, :] if not isinstance(n, int) else qparts[l][n * HG:(n + 1) * HG, :, :]
                kn = n if l else it // (ITERS // B)
                k = kparts[l][bass.ds(kn, 1), :, :]
                for row, rows in ((0, 3 * DH), (3 * DH, 2 * DH), (5 * DH, DH)):
                    for c in range(QC):
                        sp.dma_start(q_slot[u][row:row + rows, c, :, :],
                                     q[:, 0:rows, c * CH:(c + 1) * CH].rearrange("h r q -> r h q")).then_inc(S["slot_in"][u], 16)
                for row, s in ((0, 0), (1, 0), (2, 0), (3, 1), (4, 1), (5, 2)):
                    sp.dma_start(k_slot[u][row * DH:(row + 1) * DH, :],
                                 k[:, s * DH:(s + 1) * DH, :].rearrange("o d q -> (o d) q")).then_inc(S["slot_in"][u], 16)

            def max_rows(l, u, c, m):
                S = L[l]
                sp.wait_ge(S["m_ready"], m + 1)
                for s in range(MROWS):
                    sp.dma_start(q_slot[u][ROWS + s:ROWS + s + 1, c, :, :].rearrange("o h (t q) -> o (h t) q", q=P),
                                 negm[c][0:NX, s, :]).then_inc(S["m_in"][c], 16)

            def store_o(l, it, u, c):
                S = L[l]
                n = it * SLOTS + u
                sp.wait_ge(S["o_copied"], n * QC + c + 2)
                for h in range(HG):
                    sp.dma_start(numer[l][bass.ds(n * HG + h, 1), :, c * CH:(c + 1) * CH].rearrange("o d q -> (o d) q"),
                                 o_sb[c][32 * h:32 * h + DH, :]).then_inc(S["o_out"][c], 16)
                sp.dma_start(denom[l][bass.ds(n * HG, HG), c * CH:(c + 1) * CH],
                             o_sb[c][DH:P:32, :]).then_inc(S["o_out"][c], 16)

            def attention(l):
                S = L[l]
                store_parts(l, 0)
                for m in range(NQ):
                    sp.wait_ge(S["q_out"][m], 16 * PARTS * QC)
                load_slot(l, 0, 0)
                store_parts(l, 1)
                for u in range(1, SLOTS - 1):
                    load_slot(l, 0, u)
                for m in range(NQ):
                    sp.wait_ge(S["q_out"][m], 16 * PARTS * NCH)
                for c in range(1 if TAIL[l] else QC):
                    max_rows(l, 0, c, c)

                def step(it, u, last):
                    n = it * SLOTS + u
                    final = last and u == SLOTS - 1
                    if not (last and u > 0):
                        v = (u + SLOTS - 1) % SLOTS
                        sp.wait_ge(S["pv_done"], n * per_group[l] + P_RING)
                        load_slot(l, it if u == 0 else it + 1, v)
                    if TAIL[l]:
                        max_rows(l, u, 1, n * QC + 1)
                        store_o(l, it, u, 0)
                    if not final:
                        max_rows(l, (u + 1) % SLOTS, 0, (n + 1) * QC)
                    if not TAIL[l]:
                        store_o(l, it, u, 0)
                        if not final:
                            max_rows(l, (u + 1) % SLOTS, 1, (n + 1) * QC + 1)
                    store_o(l, it, u, 1)

                with sp.Fori(0, ITERS - 1) as it:
                    for u in range(SLOTS):
                        step(it, u, False)
                for u in range(SLOTS):
                    if u == 0:
                        load_output(l, 0)
                    if u == 2:
                        load_inverses(l, 0)
                    step(ITERS - 1, u, True)
                load_output(l, 1)
                load_inverses(l, 1)
                if l == 0:
                    sp.wait_ge(S["acc_biased"], TT)
                    sp.dma_start(bias_o[:, :], bbase.partition_broadcast(P)).then_inc(bias_in[1], 16)

            def load_output(l, b):
                S = L[l]
                for c in range(QC):
                    sp.wait_ge(S["o_out"][c], 80 * NG * (b + 1) + 16)
                heads = slice(b * H, (b + 1) * H)
                sp.dma_start(inv[b], denom[l][heads, :].rearrange("h (a n) -> (h a) n", n=H * N // P)).then_inc(S["den_in"][b], 16)
                for t in range(KC):
                    h0 = b * H + t * (P // DH)
                    sp.dma_start(xnT[:, t, b * N:(b + 1) * N],
                                 numer[l][h0:h0 + P // DH, :, :].rearrange("h d q -> (h d) q")).then_inc(S["num_in"][b * KC + t], 16)

            def load_inverses(l, b):
                S = L[l]
                heads = slice(b * H, (b + 1) * H)
                sp.wait_ge(S["inv_ready"], b + 1)
                sp.dma_start(inverse[l][heads, :].rearrange("h (a n) -> (h a) n", n=H * N // P), inv[b]).then_inc(S["inv_out"][b], 16)
                sp.wait_ge(S["inv_out"][b], 16)
                for t in range(KC):
                    h0 = b * H + t * (P // DH)
                    src = inverse[l][h0:h0 + P // DH, :].rearrange("h (o n) -> h o n", o=1).to_broadcast([P // DH, DH, N])
                    sp.dma_start(den[b][t], src).then_inc(S["num_in"][b * KC + t], 16)

            load_ffn0(range(0, 2))
            load_projections(0)
            load_ffn0(range(2, FT))
            for l in (0, 1):
                S = L[l]
                if l == 1:
                    sp.wait_ge(L[0]["y2_ready"], TT)
                    sp.wait_ge(L[0]["y2_evac"], TT)
                    load_projections(1)
                    load_ffn1()
                if l == 1:
                    sp.wait_ge(S["b_ready"], TT)
                    sp.dma_start(rope_cos, rcos).then_inc(rope_in, 16)
                    sp.dma_start(rope_sin, rsin).then_inc(rope_in, 16)
                attention(l)
            S = L[1]
            for t in range(TT):
                sp.wait_ge(S["y2_evac"], t + 1)
                sp.dma_start(out[t * P:(t + 1) * P, :], res[t % 4]).then_inc(S["stored"][t % 4], 16)
            for s in S["stored"]:
                sp.wait_ge(s, 16 * TT // 4)

        @block.gpsimd
        def _(pool):
            pool.memset(ident[:, :], 0.0).then_inc(const_a, 1)
            pool.memset(identb[:, :], 0.0).then_inc(const_a, 1)
            pool.memset(mask_kq[:, :], 0.0).then_inc(const_a, 1)
            pool.memset(mask_qk[:, :], 0.0).then_inc(const_a, 1)
            pool.memset(v_all[:, :, :, DH:DH + 1], 1.0).then_inc(const_a, 1)
            pool.wait_ge(const_a, 5)
            for m in (ident, identb):
                pool.affine_select(out=m[:, :], in_=m[:, :], compare_op=ALU.not_equal, fill=1.0, base=0,
                                   pattern=[[-1, P]], channel_multiplier=1).then_inc(const_b, 1)
            pool.affine_select(out=mask_kq[:, :], in_=mask_kq[:, :], compare_op=ALU.is_ge, fill=MASKED, base=0,
                               pattern=[[1, P]], channel_multiplier=-1).then_inc(const_b, 1)
            pool.affine_select(out=mask_qk[:, :], in_=mask_qk[:, :], compare_op=ALU.is_ge, fill=MASKED, base=0,
                               pattern=[[-1, P]], channel_multiplier=1).then_inc(const_b, 1)
            pool.iota(iota8u[:, :], pattern=[[1, E]], base=0, channel_multiplier=0).then_inc(iota_done, 1)
            pool.wait_ge(iota_done, 1)
            pool.tensor_copy(iota8[:, :], iota8u[:, :]).then_inc(iota_done, 1)
            for l in (0, 1):
                S = L[l]
                pool.wait_ge(bias_in[l], 16)
                for t in range(TT):
                    pool.wait_ge(S["xn_ready"], t + 1)
                    pool.tensor_tensor(acc[:, t, :], acc[:, t, :], bias_o[:, :], ALU.add).then_inc(S["acc_biased"], 1)
                for c in range(NCH):
                    for m in range(NQ):
                        rows = DH if (m == KC and l == 0) else P
                        pool.wait_ge(S["mid_done"], c * NQ + m + 1)
                        pool.tensor_tensor(part[m][0:rows, 2, :], rest[m][0:rows, :], part[m][0:rows, 1, :],
                                           ALU.subtract).then_inc(S["lo_done"], 1)
                    if c == 0:
                        pool.wait_ge(S["lo_done"], NQ)
                        for u in range(SLOTS):
                            pool.memset(k_slot[u][ROWS:ROWS + MROWS, :], 1.0).then_inc(S["v_slot_ready"], 1)
                        pool.wait_ge(S["v_slot_ready"], SLOTS)
                pool.wait_ge(S["v_done"], V_STEPS[l])

                def v_stage(it, u):
                    n = it * SLOTS + u
                    vn = n if l else it // (ITERS // B)
                    pool.tensor_copy(v_slot[u], v_all[:, vn, :, :]).then_inc(S["v_slot_ready"], 1)

                pool.wait_ge(S["lo_done"], NCH * NQ)
                for u in range(SLOTS):
                    v_stage(0, u)
                for it in range(1, ITERS):
                    for u in range(SLOTS):
                        pool.wait_ge(S["pv_done"], (it * SLOTS + u - SLOTS + 1) * per_group[l] + P_RING)
                        v_stage(it, u)
                for t in range(KC):
                    pool.wait_ge(S["num_in"][t], 16 * 2)
                    o = xnT[:, t, 0:N]
                    pool.tensor_tensor(o, o, den[0][t], ALU.mult).then_inc(S["on_ready0"], 1)

        @block.scalar
        def _(act):
            for l in (0, 1):
                S = L[l]
                def deviation(l, g):
                    act.wait_ge(L[l]["eps_done"], g + 1)
                    act.activation(std[:, g * TPC:(g + 1) * TPC], var[:, g * TPC:(g + 1) * TPC], ACT.Sqrt).then_inc(L[l]["sqrt_done"], 1)

                def copy_T(g):
                    for t in range(g * TPC, (g + 1) * TPC):
                        act.wait_ge(S["xn_T"], t + 1)
                        act.activation(xnT[:, :, t * P:(t + 1) * P], bank(t % 2).rearrange("p (k q) -> p k q", k=KC), ACT.Copy).then_inc(S["xnT_ready"], 1)

                if l == 1:
                    deviation(1, 1)
                    deviation(1, 2)
                    copy_T(0)
                    copy_T(1)
                    deviation(1, 3)
                    copy_T(2)
                    copy_T(3)
                else:
                    for g in range(NCH):
                        deviation(0, g)
                        copy_T(g)
                if l == 0:
                    def x_high(p, tokens):
                        act.activation(x_hi[:, p, :, :], xnT[:, :, tokens], ACT.Copy).then_inc(S["xhi_done"], 1)

                    x_high(0, slice(0, CH))
                    for r, js in enumerate(ROUNDS):
                        for n, j in enumerate(js):
                            act.wait_ge(S["raw_in"][j % 2], 48 * (j // 2 + 1))
                            if r:
                                act.wait_ge(S["y_ready"], TT * r)
                            for raw, hi in zip(weight_views(w_raw[:, j % 2, :], j), weight_views(w_hi[:, n, :], j)):
                                act.activation(hi, raw, ACT.Copy).then_inc(S["whi_done"], 1)
                        with act.Fori(0, NCH // 2) as i:
                            for half in range(2):
                                base = NCH * W_SLOTS * r + (2 * i + half) * len(js)
                                for n, j in enumerate(js):
                                    w = width_f(j)
                                    act.wait_ge(S["gu_ready"], base + n + 1)
                                    act.activation(sil[0:w, n % 2, :], bank(n % 2)[0:w, :], ACT.Silu).then_inc(S["silu_done"], 1)
                                    if n == 0:
                                        x_high(1 - half, bass.ds(i * CH * 2 + CH, CH) if half == 0 else bass.ds(i * (-CH * 2) + CH * 2, CH))
                else:
                    for t in range(TT):
                        act.wait_ge(S["hl_ready"], t + 1)
                        act.activation(hl[:, t, :], bank(t % 2)[:, 0:E * R + E], ACT.Copy).then_inc(S["hl_sb"], 1)
                    act.wait_ge(S["gap_done"], 1)
                    act.activation(egap, gap, ACT.Exp).then_inc(S["egap_done"], 1)
                    for t in range(TT):
                        act.wait_ge(S["hwT_ready"], t + 1)
                        act.activation(hwT[:, t, :], bank(t % 2)[:, 0:P], ACT.Copy).then_inc(S["hwT_sb"], 1)
                if l == 0:
                    act.wait_ge(S["wp_in"], 16 * 7)
                def middle(i):
                    m = i % NQ
                    rows = DH if (m == KC and l == 0) else P
                    act.wait_ge(S["rest_ready"], i + 1)
                    act.activation(part[m][0:rows, 1, :], rest[m][0:rows, :], ACT.Copy).then_inc(S["mid_done"], 1)

                for c in range(NCH):
                    for m in range(NQ):
                        i = c * NQ + m
                        rows = 2 * DH if (m == KC and l == 0) else P
                        bias = 0.0 if l else (bias_q[:, m:m + 1] if m < KC else bias_kv[:, 0:1])
                        if c:
                            act.wait_ge(S["rest_ready"], i - NQ + 1)
                        act.wait_ge(S["q_ready"], i + 1)
                        act.activation(q32[m][0:rows, :], bank(m)[0:rows, :], ACT.Identity, bias=bias).then_inc(S["q32_ready"], 1)
                        if i >= MID_LAG:
                            middle(i - MID_LAG)
                for t in range(TT if l else 0):
                    b, kt = divmod(t, KT)
                    act.wait_ge(S["v_ready"], t + 1)
                    src = bank(5 + t % 3)[:, 0:KVW[l]].rearrange("p (h d) -> p h d", h=NG)
                    act.activation(v_all[:, b * NG:(b + 1) * NG, kt, 0:DH], src, ACT.Copy).then_inc(S["v_done"], 1)
                    if t in (KT, KT + 2):
                        middle(NCH * NQ - MID_LAG + (t - KT) // 2)
                if l == 0:
                    for i in range(NCH * NQ - MID_LAG, NCH * NQ):
                        middle(i)

                items = [main_items(l == 1, c) for c in range(QC)]
                group_items = per_group[l]
                for m in range(NQ):
                    act.wait_ge(S["q_out"][m], 16 * PARTS * NCH)
                for c in range(QC):
                    act.sem_inc(S["o_out"][c], 16)
                act.sem_inc(S["p_ready"], SP_RING)

                def attend(it, last_iter):
                    base = it * (SLOTS * group_items)
                    local = 0

                    def copy_o(u, c, through):
                        n = it * SLOTS + u
                        act.wait_ge(S["pv_done"], base + through + P_RING)
                        act.wait_ge(S["o_out"][c], n * 80 + 16)
                        act.activation(o_sb[c], bank(7), ACT.Copy).then_inc(S["o_copied"], 1)

                    before = None
                    for u in range(SLOTS):
                        for c in range(QC):
                            for i, (kt, h, q0) in enumerate(items[c]):
                                act.wait_ge(S["s_ready"], base + local + 1)
                                act.wait_ge(S["pv_done"], base + local + 1)
                                act.activation(prob[local % P_RING][:, q0:CH], bank(local % SP_RING)[:, q0:CH],
                                               ACT.Exp, scale=SCALE).then_inc(S["p_ready"], 1)
                                local += 1
                                if i == 1 and before:
                                    copy_o(*before)
                                if last_iter and u == SLOTS - 1 and c == 0 and i >= P_RING and i % 2 == 0 and (i - P_RING) // 2 < KC:
                                    k = (i - P_RING) // 2
                                    act.activation(wo_hi[:, k, :], w_o[:, k, :], ACT.Copy).then_inc(S["wo_hi_done"], 1)
                            before = (u, c, local)
                    copy_o(*before)

                with act.Fori(0, ITERS - 1) as it:
                    attend(it, False)
                attend(ITERS - 1, True)

                for c in range(NCH):
                    if c < QC:
                        act.wait_ge(S["on_ready0"], KC)
                    else:
                        act.wait_ge(S["on_ready1"], KC * (c - QC + 1))
                    if c >= 2:
                        act.wait_ge(S["y2_ready"], (c - 1) * TPC)
                    act.activation(xo_hi[:, c % 2, :, :], xnT[:, :, c * CH:(c + 1) * CH], ACT.Copy).then_inc(S["xo_hi_done"], 1)
                    if l == 0 and c == 2:
                        deviation(1, 0)

        @block.vector
        def _(dve):
            made = [0]

            def chained(ins):
                ins.then_inc(dve_chain, 1)
                made[0] += 1

            def wait_chain():
                dve.wait_ge(dve_chain, made[0])

            def normalise(l, g):
                S = L[l]
                ts = range(g * TPC, (g + 1) * TPC)
                q = slice(g * TPC, (g + 1) * TPC)
                for t in ts:
                    chained(dve.bn_stats(stats[:, t, :], acc[:, t, :]))
                wait_chain()
                for t in ts:
                    chained(dve.bn_aggr(mv[:, t, :], stats[:, t, :]))
                wait_chain()
                dve.tensor_scalar(var[:, q], mv[:, q, 1], EPS, None, ALU.add).then_inc(S["eps_done"], 1)
                dve.wait_ge(S["sqrt_done"], g + 1)
                chained(dve.reciprocal(rstd[:, q], std[:, q]))
                wait_chain()
                chained(dve.tensor_tensor(nwt[:, q], rstd[:, q], rstd[:, q], ALU.mult))
                wait_chain()
                chained(dve.tensor_tensor(std[:, q], nwt[:, q], var[:, q], ALU.mult))
                wait_chain()
                chained(dve.tensor_scalar(nwt[:, q], std[:, q], -0.5, 1.5, ALU.mult, ALU.add))
                wait_chain()
                chained(dve.tensor_tensor(std[:, q], rstd[:, q], nwt[:, q], ALU.mult))
                wait_chain()
                for t in ts:
                    if t >= XN_RING[l]:
                        dve.wait_ge(S["xn_T"], t - XN_RING[l] + 1)
                    dve.tensor_scalar(xn[l][t % XN_RING[l]], acc[:, t, :], mv[:, t, 0:1], std[:, t:t + 1], ALU.subtract,
                                      ALU.mult).then_inc(S["xn_ready"], 1)

            for g in range(NCH):
                dve.wait_ge(x_in[g], 16)
                normalise(0, g)
            for l in (0, 1):
                S = L[l]
                if l == 0:
                    def x_low(p, tokens, n):
                        dve.wait_ge(S["xhi_done"], n)
                        dve.tensor_tensor(x_lo[:, p, :, :], xnT[:, :, tokens], x_hi[:, p, :, :].bitcast(F32),
                                          ALU.subtract).then_inc(S["xc_ready"], 1)

                    dve.wait_ge(S["xnT_ready"], TT)
                    x_low(0, slice(0, CH), 1)
                    for r, js in enumerate(ROUNDS):
                        for n, j in enumerate(js):
                            dve.wait_ge(S["whi_done"], 2 * (j + 1))
                            last = None
                            for raw, hi, lo in zip(weight_views(w_raw[:, j % 2, :], j), weight_views(w_hi[:, n, :], j),
                                                   weight_views(w_lo[:, n, :], j)):
                                last = dve.tensor_tensor(lo, raw, hi.bitcast(F32), ALU.subtract)
                            last.then_inc(S["w_ready"], 1)
                        with dve.Fori(0, NCH // 2) as i:
                            for half in range(2):
                                chunk = 2 * i + half
                                base = NCH * W_SLOTS * r + chunk * len(js)
                                for n, j in enumerate(js):
                                    w = width_f(j)
                                    dve.wait_ge(S["silu_done"], base + n + 1)
                                    dve.tensor_tensor(hid[0:w, n % 2, :], sil[0:w, n % 2, :], bank(2 + n % 2)[0:w, :], ALU.mult).then_inc(S["prod_done"], 1)
                                    dve.wait_ge(S["prod_done"], base + n + 1)
                                    dve.tensor_copy(h_hi[0:w, n % 2, :], hid[0:w, n % 2, :]).then_inc(S["hhi_done"], 1)
                                    dve.wait_ge(S["hhi_done"], base + n + 1)
                                    dve.tensor_tensor(h_lo[0:w, n % 2, :], hid[0:w, n % 2, :], h_hi[0:w, n % 2, :].bitcast(F32),
                                                      ALU.subtract).then_inc(S["hid_done"], 1)
                                    if n == 0:
                                        x_low(1 - half, bass.ds(i * CH * 2 + CH, CH) if half == 0 else bass.ds(i * (-CH * 2) + CH * 2, CH),
                                              NCH * r + chunk + 2)
                                for t in range(TPC):
                                    tile = chunk * TPC + t
                                    dve.wait_ge(S["acc_biased"], tile + 1)
                                    dve.wait_ge(S["y_ready"], TT * r + tile + 1)
                                    a = acc[:, bass.ds(tile, 1), :].rearrange("p o d -> p (o d)")
                                    dve.tensor_tensor(a, a, bank(4 + t), ALU.add).then_inc(S["y_evac"], 1)
                else:
                    dve.wait_ge(iota_done, 2)
                    lg = hl[:, :, E * R:E * R + E]
                    for t in range(TT):
                        dve.wait_ge(S["hl_sb"], t + 1)
                        dve.max(top[:, t, :], lg[:, t, :]).then_inc(dve_chain, 1)
                        made[0] += 1
                    dve.wait_ge(dve_chain, made[0])
                    dve.tensor_tensor(gap, top[:, :, 1], top[:, :, 0], ALU.subtract).then_inc(S["gap_done"], 1)
                    for t in range(TT):
                        dve.max_index(topi[:, t, :], top[:, t, :], lg[:, t, :]).then_inc(dve_chain, 1)
                        made[0] += 1
                    dve.wait_ge(dve_chain, made[0])
                    dve.tensor_copy(topf, topi[:, :, 0:2]).then_inc(dve_chain, 1)
                    made[0] += 1
                    dve.wait_ge(S["egap_done"], 1)
                    dve.tensor_scalar(esum, egap, 1.0, None, ALU.add).then_inc(dve_chain, 1)
                    made[0] += 1
                    dve.wait_ge(dve_chain, made[0])
                    dve.reciprocal(winv, esum).then_inc(dve_chain, 1)
                    made[0] += 1
                    dve.wait_ge(dve_chain, made[0])
                    dve.tensor_scalar(wt1, winv, 2.0, None, ALU.mult).then_inc(dve_chain, 1)
                    made[0] += 1
                    dve.wait_ge(dve_chain, made[0])
                    dve.tensor_tensor(wt2, wt1, egap, ALU.mult).then_inc(dve_chain, 1)
                    made[0] += 1
                    dve.wait_ge(dve_chain, made[0])
                    for t in range(TT):
                        dve.tensor_scalar(gate1[:, t, :], iota8[:, :], topf[:, t, 0:1], wt1[:, t:t + 1], ALU.is_equal, ALU.mult).then_inc(dve_chain, 1)
                        made[0] += 1
                        dve.tensor_scalar(gate2[:, t, :], iota8[:, :], topf[:, t, 1:2], wt2[:, t:t + 1], ALU.is_equal, ALU.mult).then_inc(dve_chain, 1)
                        made[0] += 1
                    dve.wait_ge(dve_chain, made[0])
                    dve.tensor_tensor(gate, gate1, gate2, ALU.add).then_inc(dve_chain, 1)
                    made[0] += 1
                    dve.wait_ge(dve_chain, made[0])
                    for t in range(TT):
                        g = gate[:, t, :].rearrange("p (e o) -> p e o", o=1).to_broadcast([P, E, R])
                        dve.tensor_tensor(hw[:, t, :].rearrange("p (e r) -> p e r", e=E),
                                          hl[:, t, 0:E * R].rearrange("p (e r) -> p e r", e=E), g, ALU.mult).then_inc(S["hw_done"], 1)
                    for t in range(TT):
                        dve.wait_ge(S["acc_biased"], t + 1)
                        dve.wait_ge(S["b_ready"], t + 1)
                        dve.tensor_tensor(acc[:, t, :], acc[:, t, :], bank(2 + t % 6), ALU.add).then_inc(S["b_evac"], 1)

                if l:
                    dve.wait_ge(rope_in, 32)
                def take_v(c):
                    dve.wait_ge(S["v_ready"], c + 1)
                    src = bank(5 + c % 3)[:, 0:2 * DH * TPC].rearrange("p (t d) -> p t d", t=TPC)
                    k0 = c % QC * TPC
                    dve.tensor_copy(v_all[:, c // QC, k0:k0 + TPC, 0:DH], src[:, :, DH:2 * DH]).then_inc(S["v_done"], 1)

                for c in range(NCH):
                    pos = slice(c % QC * CH, (c % QC + 1) * CH)
                    for m in range(NQ):
                        rows = DH if (m == KC and l == 0) else P
                        dve.wait_ge(S["q32_ready"], c * NQ + m + 1)
                        if c:
                            dve.wait_ge(S["q_out"][m], c * (16 * PARTS))
                        if l:
                            dve.stream_shuffle(rest[m], q32[m], swap).then_inc(dve_chain, 1)
                            made[0] += 1
                            dve.wait_ge(dve_chain, made[0])
                            dve.tensor_tensor(q32[m], q32[m], rope_cos[:, pos], ALU.mult).then_inc(dve_chain, 1)
                            dve.tensor_tensor(rest[m], rest[m], rope_sin[:, pos], ALU.mult).then_inc(dve_chain, 1)
                            made[0] += 2
                            dve.wait_ge(dve_chain, made[0])
                            dve.tensor_tensor(q32[m], q32[m], rest[m], ALU.add).then_inc(dve_chain, 1)
                            made[0] += 1
                            dve.wait_ge(dve_chain, made[0])
                        dve.tensor_copy(part[m][0:rows, 0, :], q32[m][0:rows, :]).then_inc(S["hi_done"], 1)
                        dve.wait_ge(S["hi_done"], c * NQ + m + 1)
                        dve.tensor_tensor(rest[m][0:rows, :], q32[m][0:rows, :], part[m][0:rows, 0, :], ALU.subtract).then_inc(S["rest_ready"], 1)
                        if l == 0 and c and m == 0:
                            take_v(c - 1)
                if l == 0:
                    take_v(NCH - 1)
                def maxima(n):
                    for e, (c, qt, h) in enumerate(max_items()):
                        j = n * (QC * XI) + e
                        src = bank(3 + 2 * (e % 2), 2)
                        dve.wait_ge(S["x_ready"], j + 1)
                        if qt is not None:
                            dve.tensor_reduce(maxes[c][:, h * TPC + qt:h * TPC + qt + 1], src[:, 0:max_width(l == 1, c, qt)],
                                              AX_X, ALU.max).then_inc(S["x_done"], 1)
                            continue
                        if not (isinstance(n, int) and n == 0):
                            dve.wait_ge(S["m_in"][c], n * (16 * MROWS))
                        mt = src[0:NX, 0:P]
                        dve.tensor_scalar(negm[c][0:NX, 0, :], mt, -1.0, None, ALU.mult).then_inc(S["mhi_done"], 1)
                        dve.wait_ge(S["mhi_done"], n * QC + c + 1)
                        dve.scalar_tensor_tensor(negm[c][0:NX, 1, :], mt, -1.0, negm[c][0:NX, 0, :], ALU.mult,
                                                 ALU.subtract).then_inc(S["m_ready"], 1)
                        dve.wait_ge(S["m_ready"], n * QC + c + 1)
                        dve.sem_inc(S["x_done"], 1)

                maxima(0)
                def invert(b):
                    dve.wait_ge(S["den_in"][b], 16)
                    dve.reciprocal(inv[b], inv[b]).then_inc(S["inv_ready"], 1)

                with dve.Fori(1, B * NG - 2) as n:
                    maxima(n)
                invert(0)
                maxima(B * NG - 2)
                maxima(B * NG - 1)

                def low(c):
                    dve.wait_ge(S["xo_hi_done"], c + 1)
                    dve.tensor_tensor(xo_lo[:, c % 2, :, :], xnT[:, :, c * CH:(c + 1) * CH], xo_hi[:, c % 2, :, :].bitcast(F32),
                                      ALU.subtract).then_inc(S["xo_ready"], 1)

                dve.wait_ge(S["wo_hi_done"], KC)
                dve.tensor_tensor(wo_lo, w_o[:, :, :], wo_hi.bitcast(F32), ALU.subtract).then_inc(S["wo_ready"], 1)
                low(0)
                invert(1)
                low(1)
                for half in range(QC):
                    for t in range(KC):
                        if half == 0:
                            dve.wait_ge(S["num_in"][KC + t], 16 * 2)
                        o = xnT[:, t, N + half * CH:N + (half + 1) * CH]
                        dve.tensor_tensor(o, o, den[1][t][:, half * CH:(half + 1) * CH], ALU.mult).then_inc(S["on_ready1"], 1)
                for t in range(TT):
                    dve.wait_ge(S["y2_ready"], t + 1)
                    if l == 0:
                        dve.tensor_tensor(acc[:, t, :], acc[:, t, :], bank(t % 8), ALU.add).then_inc(S["y2_evac"], 1)
                        if t in (TPC - 1, 2 * TPC - 1):
                            low(QC + t // TPC)
                        if t % TPC == TPC - 1:
                            dve.wait_ge(S["y2_evac"], t + 1)
                            normalise(1, t // TPC)
                    else:
                        if t >= 4:
                            dve.wait_ge(S["stored"][t % 4], 16 * (t // 4))
                        dve.tensor_tensor(res[t % 4], acc[:, t, :], bank(t % 8), ALU.add).then_inc(S["y2_evac"], 1)
                        if t in (TPC - 1, 2 * TPC - 1):
                            low(QC + t // TPC)

        @block.tensor
        def _(pe):
            def passes(out_, hi_w, lo_w, hi_x, lo_x, start, stop):
                pe.matmul(out_, hi_w, hi_x, start=start, stop=False)
                pe.matmul(out_, hi_w, lo_x, start=False, stop=False)
                return pe.matmul(out_, lo_w, hi_x, start=False, stop=stop)

            pe.wait_ge(const_b, 4)
            for l in (0, 1):
                S = L[l]
                if l == 1:
                    pe.wait_ge(L[0]["y2_evac"], 10)
                for t in range(TT):
                    pe.wait_ge(S["xn_ready"], t + 1)
                    if t >= 2:
                        pe.wait_ge(S["xnT_ready"], t - 1)
                    for k in range(KC):
                        last = pe.transpose(bank(t % 2)[:, k * P:(k + 1) * P], xn[l][t % XN_RING[l]][:, k * P:(k + 1) * P], ident[:, :])
                    last.then_inc(S["xn_T"], 1)
                pe.wait_ge(S["xnT_ready"], TT)
                if l == 1:
                    pe.wait_ge(L[0]["y2_evac"], TT)
                if l == 0:
                    pe.sem_inc(S["hid_done"], 1)
                    pe.sem_inc(S["y_evac"], 1)

                    def chunk_of_round(r, js, c, p):
                        base = NCH * W_SLOTS * r + c * len(js)

                        def down(n):
                            w = width_f(js[n])
                            pe.wait_ge(S["hid_done"], base + n + 2)
                            if n == 0:
                                pe.wait_ge(S["y_evac"], TT * r + c * TPC + 1)
                            for t in range(TPC):
                                q = slice(t * P, (t + 1) * P)
                                last = passes(bank(4 + t), h_hi[0:w, n % 2, q], h_lo[0:w, n % 2, q], w_hi[0:w, n, GU:GU + D],
                                              w_lo[0:w, n, GU:GU + D], n == 0, n == len(js) - 1)
                                if n == len(js) - 1:
                                    last.then_inc(S["y_ready"], 1)

                        pe.wait_ge(S["xc_ready"], NCH * r + c + 1)
                        for n, j in enumerate(js):
                            w = width_f(j)
                            pe.wait_ge(S["w_ready"], j + 1)
                            pe.wait_ge(S["hid_done"], base + max(1, n))
                            for g in range(2):
                                for k in range(KC):
                                    f0 = (2 * k + g) * P
                                    last = passes(bank(2 * g + n % 2)[0:w, :], w_hi[:, n, f0:f0 + w], w_lo[:, n, f0:f0 + w],
                                                  x_hi[:, p, k, :], x_lo[:, p, k, :], k == 0, k == KC - 1)
                            last.then_inc(S["gu_ready"], 1)
                            if n >= 1:
                                down(n - 1)
                        down(len(js) - 1)

                    for r, js in enumerate(ROUNDS):
                        with pe.Fori(0, NCH // 2) as i:
                            for half in range(2):
                                chunk_of_round(r, js, 2 * i + half, half)
                else:
                    pe.wait_ge(S["wf_in"], 16 * 4)
                    for t in range(TT):
                        if t >= 2:
                            pe.wait_ge(S["hl_sb"], t - 1)
                        for k in range(KC):
                            last = pe.matmul(bank(t % 2)[:, 0:E * R + E], xnT[:, k, t * P:(t + 1) * P], w_ar[:, k, :],
                                             start=(k == 0), stop=(k == KC - 1))
                        last.then_inc(S["hl_ready"], 1)
                    pe.wait_ge(S["hl_sb"], TT)

                    def base_product(t):
                        if t >= 6:
                            pe.wait_ge(S["b_evac"], t - 5)
                        for k in range(KC):
                            pe.matmul(bank(2 + t % 6), xnT[:, k, t * P:(t + 1) * P], w_base[:, k, :], start=(k == 0), stop=False)

                    def lora_product(t):
                        pe.wait_ge(S["hwT_sb"], t + 1)
                        pe.matmul(bank(2 + t % 6), hwT[:, t, :], w_lb, start=False, stop=True).then_inc(S["b_ready"], 1)

                    for t in range(6):
                        base_product(t)
                    for t in range(TT):
                        pe.wait_ge(S["hw_done"], t + 1)
                        if t >= 2:
                            pe.wait_ge(S["hwT_sb"], t - 1)
                        pe.transpose(bank(t % 2)[:, 0:P], hw[:, t, :], ident[:, :]).then_inc(S["hwT_ready"], 1)
                        if t >= 1:
                            lora_product(t - 1)
                        if 3 <= t < TT - 3:
                            base_product(t + 3)
                    lora_product(TT - 1)

                pe.wait_ge(S["wp_in"], 16 * (7 if l == 0 else 4))
                if l == 0:
                    pe.wait_ge(S["y_evac"], TT * len(ROUNDS) + 1)
                else:
                    pe.wait_ge(S["b_evac"], TT)
                kw = KVW[l]

                def transpose_v(c):
                    pe.wait_ge(S["q32_ready"], (c + 1) * NQ)
                    if c >= 3:
                        pe.wait_ge(S["v_done"], c - 2)
                    for t in range(TPC):
                        last = pe.transpose(bank(5 + c % 3)[:, 2 * DH * t:2 * DH * (t + 1)], q32[KC][0:2 * DH, t * P:(t + 1) * P],
                                            ident[0:2 * DH, 0:2 * DH])
                    last.then_inc(S["v_ready"], 1)

                for c in range(NCH):
                    if c:
                        pe.wait_ge(S["q32_ready"], c * NQ)
                    for m in range(NQ):
                        for k in range(KC):
                            wide = P if m < KC or l else 2 * kw
                            w = w_q[:, k, m * P:(m + 1) * P] if m < KC else w_kv[:, k, 0:wide]
                            last = pe.matmul(bank(m)[0:wide, :], w, xnT[:, k, c * CH:(c + 1) * CH],
                                             start=(k == 0), stop=(k == KC - 1))
                        last.then_inc(S["q_ready"], 1)
                        if l == 0 and c and m == 0:
                            transpose_v(c - 1)
                if l == 0:
                    transpose_v(NCH - 1)
                for t in range(TT if l else 0):
                    if t >= 3:
                        pe.wait_ge(S["v_done"], t - 2)
                    for k in range(KC):
                        last = pe.matmul(bank(5 + t % 3)[:, 0:kw], xnT[:, k, t * P:(t + 1) * P], w_kv[:, k, kw:2 * kw],
                                         start=(k == 0), stop=(k == KC - 1))
                    last.then_inc(S["v_ready"], 1)
                pe.wait_ge(S["v_done"], V_STEPS[l])
                pe.wait_ge(S["q32_ready"], NCH * NQ)

                causal = l == 1
                items = [main_items(causal, c) for c in range(QC)]
                group_items = per_group[l]
                pe.sem_inc(S["o_copied"], 1)
                pe.sem_inc(S["pv_done"], P_RING)

                XL = max_items()

                def max_pieces():
                    r = []
                    for e, (c, qt, h) in enumerate(XL):
                        w = 1 if qt is None else max_width(causal, c, qt)
                        r += [(e, k0, min(w, k0 + CH), w) for k0 in range(0, w, CH)]
                    return r

                XP = max_pieces()
                split = len(XL) - 1 - TAIL[l] if TAIL[l] else len(XL)
                tail = [p for p in XP if p[0] >= split]
                head = [p for p in XP if p[0] < split]

                def pace(pieces):
                    cost = [400 if XL[e][1] is None else w + 100 for e, k0, k1, w in pieces]
                    starts, cum = [], 0
                    for (e, k0, k1, w), c in zip(pieces, cost):
                        starts.append(cum)
                        cum += c if k1 == w else 0
                    return [a * MAX_END[l] * group_items / cum for a in starts]

                steps = pace(tail + head)

                def max_piece(n, u, piece):
                    e, k0, k1, w = piece
                    c, qt, h = XL[e]
                    dst = bank(3 + 2 * (e % 2), 2)
                    j = n * len(XL) + e
                    if k0 == 0 and not (isinstance(j, int) and j < 2):
                        pe.wait_ge(S["x_done"], j - 1 if e < len(XL) - 1 else j)
                    if qt is None:
                        pe.transpose(dst[0:NX, 0:P], maxes[c], ident[:, :]).then_inc(S["x_ready"], 1)
                        return
                    diag = causal and k1 == w
                    last = pe.matmul(dst[:, k0:k1], q_slot[u][0:ROWS, c, h, qt * P:(qt + 1) * P], k_slot[u][0:ROWS, k0:k1],
                                     start=True, stop=not diag)
                    if diag:
                        last = pe.matmul(dst[:, w - P:w], identb[:, :], mask_qk[:, :], start=False, stop=True)
                    if k1 == w:
                        last.then_inc(S["x_ready"], 1)

                def attend(it, last_iter):
                    base = it * (SLOTS * group_items)
                    pending = []
                    local = 0

                    def pv():
                        idx, u, c, kt, h, q0, nkt = pending.pop(0)
                        pe.wait_ge(S["p_ready"], base + idx + 1 + SP_RING)
                        if kt == 0 and h == 0:
                            pe.wait_ge(S["o_copied"], (it * SLOTS + u) * QC + c + 1)
                        mm = pe.matmul(bank(7)[32 * h:32 * h + DH + 1, q0:CH], v_slot[u][:, kt, :], prob[idx % P_RING][:, q0:CH],
                                       start=(kt == 0), stop=(kt == nkt - 1), tile_position=(0, 32 * h))
                        mm.then_inc(S["pv_done"], 1)

                    for u in range(SLOTS):
                        n = it * SLOTS + u
                        has_next = not (last_iter and u == SLOTS - 1)
                        v = (u + 1) % SLOTS
                        pe.wait_ge(S["v_slot_ready"], n + 1 + SLOTS)
                        done = 0
                        i_g = 0
                        for c in range(QC):
                            nkt = len(items[c]) // HG
                            for i, (kt, h, q0) in enumerate(items[c]):
                                if i == 0:
                                    pe.wait_ge(S["m_in"][c], (n + 1) * (16 * MROWS))
                                slot = local % SP_RING
                                free = local if local >= SP_RING else first_free[local]
                                pe.wait_ge(S["p_ready"], base + free + 1)
                                diag = causal and kt >= TPC * c
                                mm = pe.matmul(bank(slot)[:, q0:CH], k_slot[u][0:ROWS + MROWS, kt * P:(kt + 1) * P],
                                               q_slot[u][0:ROWS + MROWS, c, h, q0:CH], start=True, stop=not diag)
                                if diag:
                                    mm = pe.matmul(bank(slot)[:, q0:q0 + P], identb[:, :], mask_kq[:, :], start=False, stop=True)
                                mm.then_inc(S["s_ready"], 1)
                                pending.append((local, u, c, kt, h, q0, nkt))
                                local += 1
                                i_g += 1
                                while done < len(tail + head if has_next else tail) and steps[done] < i_g:
                                    if done < len(tail):
                                        max_piece(n, u, tail[done])
                                    else:
                                        if done == len(tail):
                                            itv = it if u + 1 < SLOTS else it + 1
                                            pe.wait_ge(S["slot_in"][v], (itv + 1) * (16 * 12))
                                        max_piece(n + 1, v, head[done - len(tail)])
                                    done += 1
                                if len(pending) > LAG:
                                    pv()
                    while pending:
                        pv()

                total = SLOTS * group_items
                first_free = []
                for s in range(SP_RING):
                    lastuse = max(i for i in range(total) if i % SP_RING == s) - total
                    first_free.append(lastuse + SP_RING)

                pe.wait_ge(S["slot_in"][0], 16 * 12)
                pe.wait_ge(S["v_slot_ready"], SLOTS)
                for piece in head:
                    max_piece(0, 0, piece)
                with pe.Fori(0, ITERS - 1) as it:
                    attend(it, False)
                attend(ITERS - 1, True)

                pe.wait_ge(S["o_copied"], B * NG * QC + 1)
                pe.wait_ge(S["wo_ready"], 1)
                for t in range(TT):
                    c, q = t // TPC, slice(t % TPC * P, (t % TPC + 1) * P)
                    pe.wait_ge(S["xo_ready"], c + 1)
                    if t >= 8:
                        pe.wait_ge(S["y2_evac"], t - 7)
                    for k in range(KC):
                        last = passes(bank(t % 8), xo_hi[:, c % 2, k, q], xo_lo[:, c % 2, k, q], wo_hi[:, k, :], wo_lo[:, k, :], k == 0, k == KC - 1)
                    last.then_inc(S["y2_ready"], 1)


def kernel(**inputs):
    import numpy as _np
    import concourse.bacc as _bacc
    from concourse import mybir as _mybir
    from concourse.bass_utils import run_bass_kernel_spmd as _run

    def flat(name):
        return _np.ascontiguousarray(inputs[name])

    lb = flat("L1_ffn_lora_B")
    laid = {
        "x": flat("L0_attn_x").reshape(T, D),
        "wq0": flat("L0_attn_Wq"), "bq0": _np.ascontiguousarray(flat("L0_attn_bq").reshape(KC, P).T), "wk0": flat("L0_attn_Wk"), "bk0": flat("L0_attn_bk"),
        "wv0": flat("L0_attn_Wv"), "bv0": flat("L0_attn_bv"), "wo0": flat("L0_attn_Wo"), "bo0": flat("L0_attn_bo"),
        "wgu": _np.ascontiguousarray(flat("L0_ffn_w_gate_up").T), "wdn": _np.ascontiguousarray(flat("L0_ffn_w_down").T),
        "wq1": flat("L1_attn_Wq"), "wk1": flat("L1_attn_Wk"), "wv1": flat("L1_attn_Wv"), "wo1": flat("L1_attn_Wo"),
        "wbase": _np.ascontiguousarray(flat("L1_ffn_W_base").T), "bbase": flat("L1_ffn_b_base"),
        "wrt": _np.ascontiguousarray(flat("L1_ffn_W_router").T),
        "la": _np.ascontiguousarray(flat("L1_ffn_lora_A").reshape(E * R, D).T),
        "lb": _np.ascontiguousarray(lb.transpose(0, 2, 1)).reshape(E * R, D),
    }
    freq = (_np.float32(1.0) / _np.float32(10000.0) ** (_np.arange(0, DH, 2, dtype=_np.float32) / _np.float32(DH))).astype(_np.float32)
    angle = (_np.arange(N, dtype=_np.float32)[None, :] * _np.tile(_np.repeat(freq, 2), P // DH)[:, None]).astype(_np.float32)
    sign = _np.where(_np.arange(P) % 2 == 0, -1.0, 1.0).astype(_np.float32)
    laid["rcos"] = _np.cos(angle).astype(_np.float32)
    laid["rsin"] = (_np.sin(angle) * sign[:, None]).astype(_np.float32)
    nc = _bacc.Bacc("TRN2", target_bir_lowering=False, num_devices=1)
    arrays, args = {}, []
    for name, a in laid.items():
        arrays[f"in_{name}"] = a
        args.append(nc.dram_tensor(f"in_{name}", a.shape, _mybir.dt.from_np(a.dtype), kind="ExternalInput").ap())
    args.append(nc.dram_tensor("out_0", (T, D), F32, kind="ExternalOutput").ap())
    build(nc, *args)
    r = _run(nc, [arrays], core_ids=[0])
    return r.results[0]["out_0"].reshape(B, N, D)
```
